# Optimizing a Trainium2 kernel written in Bass

```python
import numpy as np
import jax
import jax.numpy as jnp

def _softmax(x, axis=-1):
    return jax.nn.softmax(x, axis=axis)

def _gelu(x):
    return jax.nn.gelu(x, approximate=True)

def _silu(x):
    return jax.nn.silu(x)

def _sigmoid(x):
    return jax.nn.sigmoid(x)

def _layernorm(x, axis=-1, eps=1e-05):
    m = jnp.mean(x, axis=axis, keepdims=True)
    v = jnp.var(x, axis=axis, keepdims=True)
    return (x - m) / jnp.sqrt(v + eps)

def _scatter_add(tgt, idx, src, axis=0):
    return tgt.at[idx].add(src)

def _segment_sum(src, seg, n):
    return jax.ops.segment_sum(src, seg, n)
kernel_name = 'mk_gnn_ffn_d1_gnn_r8_796120'

def setup_inputs(seed: int=0):
    np.random.seed(seed)
    _w = jnp.asarray

    def _rec_inputs():
        import jax
        import jax.numpy as jnp
        _gk = jax.random.key(seed)
        x = -0.0003713 + 1 * jax.random.normal(jax.random.fold_in(_gk, 1), (6250, 256), jnp.float32)
        _s = jax.random.randint(jax.random.fold_in(_gk, 2), (100000,), 0, 6250, jnp.int32)
        _d = jax.random.randint(jax.random.fold_in(_gk, 3), (100000,), 0, 6250, jnp.int32)
        _loop = jnp.arange(6250, dtype=jnp.int32)
        src = jnp.concatenate([_s, _d, _loop])
        dst = jnp.concatenate([_d, _s, _loop])
        _o = jnp.argsort(dst, stable=True)
        src = src[_o]
        dst = dst[_o]
        edge_weight = jax.random.uniform(jax.random.fold_in(_gk, 12), (206250,), jnp.float32, 0.0, 1)
        return (x, src, dst, edge_weight)
    x, src, dst, edge_weight = _rec_inputs()

    def _L0_gnn_setup():
        import jax, jax.numpy as jnp
        import numpy as np
        N = 6250
        E = 100000
        D_IN, D_HID, D_OUT = (256, 512, 256)
        LN_EPS = 1e-05

        def _layer_norm(x, g, b):
            mu = jnp.mean(x, axis=-1, keepdims=True)
            var = jnp.mean(jnp.square(x - mu), axis=-1, keepdims=True)
            return (x - mu) * jax.lax.rsqrt(var + LN_EPS) * g + b
        key = jax.random.key(seed)
        ks = jax.random.split(key, 8)
        return {'v': jax.random.normal(ks[0], (N, D_IN), dtype=jnp.float32), 'edge_weight': jax.random.uniform(ks[1], (E,), dtype=jnp.float32), 'epsilon': jnp.zeros((1, 1), dtype=jnp.float32), 'w1': jax.random.normal(ks[2], (D_HID, D_IN), dtype=jnp.float32) * (1.0 / np.sqrt(D_IN)), 'b1': jnp.zeros((D_HID,), dtype=jnp.float32), 'g1': jnp.ones((D_HID,), dtype=jnp.float32), 'beta1': jnp.zeros((D_HID,), dtype=jnp.float32), 'w2': jax.random.normal(ks[3], (D_OUT, D_HID), dtype=jnp.float32) * (1.0 / np.sqrt(D_HID)), 'b2': jnp.zeros((D_OUT,), dtype=jnp.float32), 'g2': jnp.ones((D_OUT,), dtype=jnp.float32), 'beta2': jnp.zeros((D_OUT,), dtype=jnp.float32), 'src': jax.random.randint(ks[4], (E,), 0, N, dtype=jnp.int32), 'dst': jax.random.randint(ks[5], (E,), 0, N, dtype=jnp.int32)}
    _L0_gnn_all = _L0_gnn_setup()
    _L0_gnn_in = {k: v for k, v in _L0_gnn_all.items() if k in ('epsilon', 'w1', 'b1', 'g1', 'beta1', 'w2', 'b2', 'g2', 'beta2')}
    del _L0_gnn_all

    def _L0_ffn_setup():
        import jax, jax.numpy as jnp
        import numpy as np
        TOP_K = 2
        LN_EPS = 1e-05
        key = jax.random.key(seed)
        ks = jax.random.split(key, 8)
        B, S, D, E, H = (16, 1024, 256, 8, 1024)
        x = jax.random.normal(ks[0], (B, S, D), dtype=jnp.float32)
        Wr = jax.random.normal(ks[1], (D, E), dtype=jnp.float32) * 0.1
        br = jnp.zeros((E,), dtype=jnp.float32)
        ln_g = jnp.ones((E, D), dtype=jnp.float32)
        ln_b = jnp.zeros((E, D), dtype=jnp.float32)
        W1 = jax.random.normal(ks[2], (E, D, H), dtype=jnp.float32) * (1.0 / np.sqrt(D))
        b1 = jnp.zeros((E, H), dtype=jnp.float32)
        W2 = jax.random.normal(ks[3], (E, H, D), dtype=jnp.float32) * (1.0 / np.sqrt(H))
        b2 = jnp.zeros((E, D), dtype=jnp.float32)
        return {'x': x, 'Wr': Wr, 'br': br, 'ln_g': ln_g, 'ln_b': ln_b, 'W1': W1, 'b1': b1, 'W2': W2, 'b2': b2}
    _L0_ffn_all = _L0_ffn_setup()
    _L0_ffn_in = {k: v for k, v in _L0_ffn_all.items() if k in ('Wr', 'br', 'ln_g', 'ln_b', 'W1', 'b1', 'W2', 'b2')}
    del _L0_ffn_all
    return {'x': x, 'src': src, 'dst': dst, 'edge_weight': edge_weight, 'L0_gnn_epsilon': _L0_gnn_in['epsilon'], 'L0_gnn_w1': _L0_gnn_in['w1'], 'L0_gnn_b1': _L0_gnn_in['b1'], 'L0_gnn_g1': _L0_gnn_in['g1'], 'L0_gnn_beta1': _L0_gnn_in['beta1'], 'L0_gnn_w2': _L0_gnn_in['w2'], 'L0_gnn_b2': _L0_gnn_in['b2'], 'L0_gnn_g2': _L0_gnn_in['g2'], 'L0_gnn_beta2': _L0_gnn_in['beta2'], 'L0_ffn_Wr': _L0_ffn_in['Wr'], 'L0_ffn_br': _L0_ffn_in['br'], 'L0_ffn_ln_g': _L0_ffn_in['ln_g'], 'L0_ffn_ln_b': _L0_ffn_in['ln_b'], 'L0_ffn_W1': _L0_ffn_in['W1'], 'L0_ffn_b1': _L0_ffn_in['b1'], 'L0_ffn_W2': _L0_ffn_in['W2'], 'L0_ffn_b2': _L0_ffn_in['b2']}

def reference(x, src, dst, edge_weight, L0_gnn_epsilon, L0_gnn_w1, L0_gnn_b1, L0_gnn_g1, L0_gnn_beta1, L0_gnn_w2, L0_gnn_b2, L0_gnn_g2, L0_gnn_beta2, L0_ffn_Wr, L0_ffn_br, L0_ffn_ln_g, L0_ffn_ln_b, L0_ffn_W1, L0_ffn_b1, L0_ffn_W2, L0_ffn_b2):
    import jax
    import jax.numpy as jnp

    def _L0_gnn_ref(v, edge_weight, epsilon, w1, b1, g1, beta1, w2, b2, g2, beta2, src, dst):
        import jax, jax.numpy as jnp
        import numpy as np
        N = 6250
        E = 100000
        D_IN, D_HID, D_OUT = (256, 512, 256)
        LN_EPS = 1e-05

        def _layer_norm(x, g, b):
            mu = jnp.mean(x, axis=-1, keepdims=True)
            var = jnp.mean(jnp.square(x - mu), axis=-1, keepdims=True)
            return (x - mu) * jax.lax.rsqrt(var + LN_EPS) * g + b
        msgs = v[src] * edge_weight[:, None]
        agg = jax.ops.segment_sum(msgs, dst, num_segments=v.shape[0])
        h = agg + epsilon * v
        h = jax.nn.relu(_layer_norm(h @ w1.T + b1, g1, beta1))
        h = jax.nn.relu(_layer_norm(h @ w2.T + b2, g2, beta2))
        return h

    def _L0_ffn_ref(x, Wr, br, ln_g, ln_b, W1, b1, W2, b2):
        import jax, jax.numpy as jnp
        import numpy as np
        TOP_K = 2
        LN_EPS = 1e-05
        B, S, D = x.shape
        N = B * S
        xt = x.reshape(N, D)
        logits = xt @ Wr + br
        probs = jax.nn.softmax(logits, axis=-1)
        top_p, top_idx = jax.lax.top_k(probs, TOP_K)
        weights = top_p / top_p.sum(axis=-1, keepdims=True)
        mu = xt.mean(axis=-1, keepdims=True)
        var = ((xt - mu) ** 2).mean(axis=-1, keepdims=True)
        xn = (xt - mu) * jax.lax.rsqrt(var + LN_EPS)
        xe = xn[None, :, :] * ln_g[:, None, :] + ln_b[:, None, :]
        h = jax.nn.gelu(jnp.einsum('end,edh->enh', xe, W1) + b1[:, None, :], approximate=False)
        y = jnp.einsum('enh,ehd->end', h, W2) + b2[:, None, :]
        y_tok = jnp.transpose(y, (1, 0, 2))
        sel = jnp.take_along_axis(y_tok, top_idx[:, :, None], axis=1)
        out = (weights[:, :, None] * sel).sum(axis=1)
        return out.reshape(B, S, D)
    x = x + _L0_gnn_ref(_layernorm(x, axis=-1), edge_weight, L0_gnn_epsilon, L0_gnn_w1, L0_gnn_b1, L0_gnn_g1, L0_gnn_beta1, L0_gnn_w2, L0_gnn_b2, L0_gnn_g2, L0_gnn_beta2, src, dst)
    x = x + _L0_ffn_ref(_layernorm(x, axis=-1)[None], L0_ffn_Wr, L0_ffn_br, L0_ffn_ln_g, L0_ffn_ln_b, L0_ffn_W1, L0_ffn_b1, L0_ffn_W2, L0_ffn_b2)[0]
    return x

_drawn_inputs = setup_inputs


def setup_inputs(seed=0):
    import zlib

    import numpy as np

    out = dict(_drawn_inputs(seed))
    spreads = {'L0_gnn_b1': (0.0, 0.1),
     'L0_gnn_g1': (1.0, 0.2),
     'L0_gnn_beta1': (0.0, 0.1),
     'L0_gnn_b2': (0.0, 0.1),
     'L0_gnn_g2': (1.0, 0.2),
     'L0_gnn_beta2': (0.0, 0.1),
     'L0_ffn_br': (0.0, 0.1),
     'L0_ffn_ln_g': (1.0, 0.2),
     'L0_ffn_ln_b': (0.0, 0.1),
     'L0_ffn_b1': (0.0, 0.1),
     'L0_ffn_b2': (0.0, 0.1)}
    factors = {}
    for name, (base, spread) in spreads.items():
        noise = np.random.default_rng([zlib.crc32(name.encode()), seed]).standard_normal(out[name].shape)
        drawn = base * np.exp(spread * noise) if base else spread * noise
        out[name] = jnp.asarray(drawn.astype(out[name].dtype))
    for name, factor in factors.items():
        out[name] = (out[name] * factor).astype(out[name].dtype)
    return out
```

```python
from contextlib import ExitStack

import concourse.bass as bass
from concourse import mybir

P = 128
F32 = mybir.dt.float32
I32 = mybir.dt.int32
ALU = mybir.AluOpType
ACT = mybir.ActivationFunctionType
AX_X = mybir.AxisListType.X
DVE = mybir.EngineType.DVE
LN_EPS = 1e-5
RING = 16
HALF = RING // 2
SELS = 4
GROUP = 7
ROUTED = 2


class Chain:

    def __init__(self, eng, sem):
        self.eng, self.sem, self.n, self.loop = eng, sem, 0, None

    def value(self):
        if self.loop is None:
            return self.n
        i, start, per = self.loop
        return i * per + self.n

    def __call__(self, ins):
        self.n += 1
        ins.then_inc(self.sem, 1)
        self.eng.wait_ge(self.sem, self.value())

    def enter(self, i, per):
        self.loop = (i, self.n, per)

    def leave(self, passes):
        _, start, per = self.loop
        assert self.n - start == per, (self.n - start, per)
        self.n, self.loop = start + per * passes, None


def gnn_moe(nc, x, src_rows, dst_rows, weight_rows, src_cols, dst_cols, weight_cols, epsilon,
            w1t, w2t, gnn_rows, g1t, beta1t, wr, br, ln_gt, ln_bt, expert_w1, expert_w2,
            expert_bias, consts, out):
    NODES, D = x.shape
    NT = NODES // P
    NG = NT // GROUP
    ET = src_rows.shape[0]
    STEPS = ET + NT - 1
    PASSES = STEPS // RING
    HID = w1t.shape[1]
    DC, HC = D // P, HID // P
    E, _, FF = expert_w1.shape
    FC = FF // P
    SLOT_TILES = (ROUTED * NODES + E * (P - 1)) // P
    BOUND = 512
    assert ET % RING == 0 and STEPS % RING == 0 and NG * GROUP == NT and D == 256 and FF == 1024

    x_scratch = nc.dram_tensor("normed_nodes", (NODES, D), F32, kind="Internal").ap()
    x1_scratch = nc.dram_tensor("after_gnn", (NODES, D), F32, kind="Internal").ap()
    slot_in = nc.dram_tensor("slot_inputs", (SLOT_TILES * P, D), F32, kind="Internal").ap()
    slot_out = nc.dram_tensor("slot_outputs", (SLOT_TILES * P, D), F32, kind="Internal").ap()

    with ExitStack() as ctx:
        def sb(name, shape, dt=F32):
            return ctx.enter_context(nc.sbuf_tensor(name, shape, dt))

        def sem(name):
            return ctx.enter_context(nc.semaphore(name))

        region_a = sb("region_a", [P, E * DC * FF])
        region_b = sb("region_b", [P, E * FC * D])
        agg = sb("agg", [P, NT * D])
        const = sb("const", [P, 4 * P + 1])
        ident, before, iota, ones = (const[:, n * P:(n + 1) * P] for n in range(4))
        bank = [ctx.enter_context(nc.psum_tensor(f"bank{n}", [P, BOUND], F32)) for n in range(8)]

        xn = region_a[:, 0:NT * D]

        used = [0]

        def carve(n, dt=F32):
            at = used[0]
            used[0] += n
            assert used[0] <= E * FC * D
            view = region_b[:, at:at + n]
            return view if dt is F32 else view.bitcast(dt)

        w1_sb = sb("w1_sb", [P, DC * HID])
        w2_sb = sb("w2_sb", [P, HC * D])
        rows_sb = sb("rows_sb", [P, HID + 3 * D])
        b1_row, b2_row, g2_row, beta2_row = (rows_sb[:, a:b] for a, b in (
            (0, HID), (HID, HID + D), (HID + D, HID + 2 * D), (HID + 2 * D, HID + 3 * D)))
        small = sb("small", [P, 2 * HC + DC * E + E + 2 * E * DC + 1])
        at = 0
        views = []
        for width in (HC, HC, DC * E, E, E * DC, E * DC, 1):
            views.append(small[:, at:at + width])
            at += width
        g1_col, beta1_col, wr_sb, br_row, ln_g_col, ln_b_col, eps_col = views
        logits = sb("logits", [P, NT * E])
        share = sb("share", [P, ROUTED * NT])
        place = sb("place", [P, ROUTED * NT], I32)
        tile_expert = sb("tile_expert", [P, P], I32)
        zeros = sb("zeros", [P, D])

        COLS = STEPS + 4
        src_sb, lo_sb = carve(COLS, I32), carve(COLS, I32)
        rel_sb, wgt_sb, dstf = carve(COLS), carve(COLS), carve(COLS)
        dst_sb = carve(ET, I32)
        gathered = carve(RING * D).rearrange("p (r d) -> p r d", r=RING)
        select = carve(SELS * P).rearrange("p (r d) -> p r d", r=SELS)
        staged = carve(RING, I32)
        border = carve(5 * P)
        border_rows = carve(3 * P)
        border_at = carve(1, I32)
        stats = carve(GROUP * 6)
        moments = carve(GROUP * 2)
        rstd = carve(GROUP)

        used[0] = 0
        x_group, hidden, second = carve(GROUP * D), carve(GROUP * HID), carve(GROUP * D)
        normed = carve(GROUP * D)
        h0 = carve(2 * D).rearrange("p (r d) -> p r d", r=2)
        h0t = carve(2 * D).rearrange("p (r d) -> p r d", r=2)
        act1t = carve(2 * HID).rearrange("p (r d) -> p r d", r=2)
        yt = carve(2 * D).rearrange("p (r d) -> p r d", r=2)
        g_stats, g_moments, g_rstd = carve(GROUP * 6), carve(GROUP * 2), carve(GROUP)
        scores, onehot0, onehot1, both, work, running, other = (carve(NT * E) for _ in range(7))
        per_token = [carve(NT) for _ in range(4)]
        ahead = [carve(E) for _ in range(5)]
        ends = carve(P * E)
        expert_f = carve(P)
        row_stage = second.rearrange("p (k d) -> p k d", k=GROUP)
        place_stage = carve(GROUP * ROUTED, I32)

        used_agg = [0]

        def carve_agg(n, dt=F32):
            at = used_agg[0]
            used_agg[0] += n
            assert used_agg[0] <= NT * D
            view = agg[:, at:at + n]
            return view if dt is F32 else view.bitcast(dt)

        x_in = carve_agg(2 * D).rearrange("p (r d) -> p r d", r=2)
        xt = carve_agg(2 * D).rearrange("p (r d) -> p r d", r=2)
        bias = carve_agg(2 * (FF + D)).rearrange("p (r d) -> p r d", r=2)
        hid, hid_t = carve_agg(FF), carve_agg(FF)
        y_sb = carve_agg(2 * D).rearrange("p (r d) -> p r d", r=2)
        first_y = carve_agg(GROUP * D).rearrange("p (k d) -> p k d", k=GROUP)
        second_y = carve_agg(GROUP * D).rearrange("p (k d) -> p k d", k=GROUP)
        x1_group = carve_agg(GROUP * D)
        slot_stage = carve_agg(GROUP * ROUTED, I32)
        w1_all = region_a
        w2_all = region_b

        s_const = sem("const_loaded")
        s_edges = sem("edges_loaded")
        s_x = sem("x_loaded")
        s_dve = sem("dve_step")
        s_sqrt_in = sem("variance_ready")
        s_sqrt = sem("deviation_ready")
        s_xn = sem("normed_ready")
        s_xn_stored = sem("normed_stored")
        s_dstf = sem("dst_float_ready")
        s_bcast = sem("first_dst_spread")
        s_border_at = sem("border_tile_known")
        s_border_rows = sem("border_rows_gathered")
        s_border_in = sem("border_rows_ready")
        s_border_t = sem("border_rows_turned")
        s_plan = sem("plan_ready")
        s_staged = sem("indices_staged")
        s_gather = [sem(f"gathered{n}") for n in range(RING)]
        s_select = sem("selection_ready")
        s_partial = sem("partial_sum_ready")
        s_added = sem("partial_sum_added")
        s_claimed = sem("slots_claimed")

        s_param = sem("parameters_loaded")
        s_zero = sem("zero_tile_ready")
        s_cleared = sem("slots_cleared")
        s_xg = sem("x_group_loaded")
        s_xg_free = sem("x_group_used")
        s_x1 = sem("x1_group_ready")
        s_x1_stored = sem("x1_stored")
        s_h0, s_h0t, s_h0c, s_m1, s_h1 = (sem(n) for n in ("h0_ready", "h0_turned", "h0_copied", "product1_ready", "product1_taken"))
        s_var, s_dev = sem("group_variance_ready"), sem("group_deviation_ready")
        s_z1, s_z1t, s_a1, s_m2, s_h2 = (sem(n) for n in ("z1_ready", "z1_turned", "act1_ready", "product2_ready", "product2_taken"))
        s_y, s_yt, s_yc, s_lg, s_lt = (sem(n) for n in ("y_ready", "y_turned", "y_copied", "logits_ready", "logits_taken"))
        s_shift, s_exp, s_both, s_count, s_routed = (sem(n) for n in ("shifted_ready", "exponentials_ready", "choice_ready", "counts_ready", "routing_ready"))
        s_row = sem("row_tile_staged")
        s_sent = [sem(f"rows_sent{k}") for k in range(GROUP)]
        s_wait = sem("pool_waited")
        s_settle = sem("dve_settled")
        s_weights = sem("expert_weights_loaded")
        s_xin = [sem(f"slot_rows_loaded{r}") for r in range(2)]
        s_bias = [sem(f"bias_loaded{r}") for r in range(2)]
        s_xt, s_xs, s_f1, s_hb, s_ht, s_ge, s_f2, s_ys = (sem(n) for n in (
            "slot_rows_turned", "slot_rows_scaled", "up_ready", "up_biased", "up_turned", "gelu_ready", "down_ready", "down_biased"))
        s_y_free = sem("slot_output_stored_and_free")
        s_y_stored = [sem(f"slot_output_stored{r}") for r in range(2)]
        s_idx = sem("slots_staged")
        s_pair = [sem(f"pair_gathered{k}") for k in range(GROUP)]
        s_x1g = sem("x1_group_loaded")
        s_half = sem("first_output_added")
        s_sum = sem("sum_ready")
        s_out = sem("out_stored")

        block = ctx.enter_context(nc.Block())

        def group_rows(dram, g):
            return dram[bass.ds(g * (GROUP * P), GROUP * P), :].rearrange("(t p) d -> p t d", p=P)

        def tiled(view):
            return view.rearrange("p (t d) -> p t d", d=D)

        PER_GROUP = 15
        LOOKED = 2
        PAIRS = (SLOT_TILES - LOOKED) // 2

        @block.sync
        def _(sp):
            for src, dst in ((dst_cols, dst_sb[:, 0:ET]), (src_cols, src_sb[:, 0:ET]), (weight_cols, wgt_sb[:, 0:ET])):
                sp.dma_start(dst, src).then_inc(s_edges, 16)
            sp.dma_start(const[:, :], consts).then_inc(s_const, 16)
            sp.dma_start(tiled(xn), x.rearrange("(t p) d -> p t d", p=P)).then_inc(s_x, 16)
            for g in range(NG):
                sp.wait_ge(s_xn, g + 1)
                sp.dma_start(group_rows(x_scratch, g), tiled(xn[:, g * GROUP * D:(g + 1) * GROUP * D])).then_inc(s_xn_stored, 16)
            params = ((w1_sb[:, :].rearrange("p (c n) -> p c n", c=DC), w1t.rearrange("(c p) n -> p c n", p=P)),
                      (w2_sb[:, :].rearrange("p (c n) -> p c n", c=HC), w2t.rearrange("(c p) n -> p c n", p=P)),
                      (rows_sb[:, :], gnn_rows.to_broadcast([P, HID + 3 * D])), (g1_col, g1t), (beta1_col, beta1t),
                      (wr_sb.rearrange("p (c n) -> p c n", c=DC), wr.rearrange("(c p) n -> p c n", p=P)),
                      (br_row, br.to_broadcast([P, E])), (ln_g_col, ln_gt), (ln_b_col, ln_bt),
                      (eps_col, epsilon.to_broadcast([P, 1])))
            for dst, src in params:
                sp.dma_start(dst, src).then_inc(s_param, 16)
            sp.wait_ge(s_zero, 1)
            sp.dma_start(slot_in.rearrange("(t p) d -> p t d", p=P),
                         zeros[:, :].rearrange("p (t d) -> p t d", t=1).to_broadcast([P, SLOT_TILES, D])).then_inc(s_cleared, 16)

            sp.wait_ge(s_added, SELS + STEPS)
            sp.dma_start(tiled(x_group), group_rows(x, 0)).then_inc(s_xg, 16)
            with sp.Fori(0, NG - 1) as g:
                sp.wait_ge(s_x1, g + 1)
                sp.dma_start(group_rows(x1_scratch, g), tiled(x_group)).then_inc(s_x1_stored, 16)
                sp.wait_ge(s_x1_stored, (g + 1) * 16)
                sp.wait_ge(s_xg_free, g + 1)
                sp.dma_start(tiled(x_group), group_rows(x, g + 1)).then_inc(s_xg, 16)
            sp.wait_ge(s_x1, NG)
            sp.dma_start(group_rows(x1_scratch, NG - 1), tiled(x_group)).then_inc(s_x1_stored, 16)

            sp.wait_ge(s_routed, 1)
            for e in range(E):
                sp.dma_start(w1_all[:, e * DC * FF:(e + 1) * DC * FF].rearrange("p (c n) -> p c n", c=DC),
                             expert_w1[e].rearrange("(c p) n -> p c n", p=P)).then_inc(s_weights, 16)
            for k in range(GROUP):
                sp.wait_ge(s_sent[k], 16 * ROUTED * NG)
            sp.wait_ge(s_x1_stored, 16 * NG)
            for e in range(E):
                sp.dma_start(w2_all[:, e * FC * D:(e + 1) * FC * D].rearrange("p (c n) -> p c n", c=FC),
                             expert_w2[e].rearrange("(c p) n -> p c n", p=P)).then_inc(s_weights, 16)

            def load_rows(j, r):
                sp.dma_start(x_in[:, r, :], slot_in[bass.ds(j * P, P), :]).then_inc(s_xin[r], 16)

            def load_bias(j, r):
                e = sp.value_load(tile_expert[0:1, bass.ds(j, 1)], min_val=0, max_val=E - 1)
                sp.dma_start(bias[:, r, :], expert_bias[bass.ds(e, 1), :].to_broadcast([P, FF + D])).then_inc(s_bias[r], 16)

            def slot_tile(j, r, m, more):
                if more:
                    sp.wait_ge(s_xt, j + 1)
                    load_rows(j + LOOKED, r)
                sp.wait_ge(s_ys, j + 1)
                sp.dma_start(slot_out[bass.ds(j * P, P), :], y_sb[:, r, :]).then_inc(s_y_stored[r], 16)
                if more:
                    load_bias(j + LOOKED, r)
                sp.wait_ge(s_y_stored[r], m * 16 + 16)
                sp.sem_inc(s_y_free, 1)

            for j in range(LOOKED):
                load_rows(j, j)
                load_bias(j, j)
            with sp.Fori(0, PAIRS) as i:
                for r in range(2):
                    slot_tile(i * 2 + r, r, i, True)
            for j in range(2 * PAIRS, SLOT_TILES):
                slot_tile(j, j % 2, j // 2, j + LOOKED < SLOT_TILES)

            def load_x1(g):
                sp.dma_start(tiled(x1_group), group_rows(x1_scratch, g)).then_inc(s_x1g, 16)

            load_x1(0)
            with sp.Fori(0, NG - 1) as g:
                sp.wait_ge(s_sum, (g + 1) * GROUP)
                sp.dma_start(group_rows(out, g), tiled(x1_group)).then_inc(s_out, 16)
                sp.wait_ge(s_out, (g + 1) * 16)
                load_x1(g + 1)
            sp.wait_ge(s_sum, NT)
            sp.dma_start(group_rows(out, NG - 1), tiled(x1_group)).then_inc(s_out, 16)
            sp.wait_ge(s_out, 16 * NG)

        @block.scalar
        def _(act):
            for g in range(NG):
                act.wait_ge(s_sqrt_in, g + 1)
                nc.scalar.activation(rstd[:, :], moments[:, 1::2], ACT.Sqrt).then_inc(s_sqrt, 1)
            act.wait_ge(s_plan, 1)
            with act.Fori(0, PASSES) as i:
                for h in range(2):
                    act.wait_ge(s_partial, i * RING + (h + 1) * HALF)
                    nc.scalar.copy(staged[:, h * HALF:(h + 1) * HALF],
                                   src_sb[:, bass.ds(i * RING + h * HALF, HALF)]).then_inc(s_staged, 1)

            act.wait_ge(s_param, 160)
            with act.Fori(0, NG) as g:
                def deviation(n):
                    act.wait_ge(s_var, g * 4 + n + 1)
                    nc.scalar.activation(g_rstd, g_moments[:, 1::2], ACT.Sqrt).then_inc(s_dev, 1)

                for k in range(GROUP):
                    act.wait_ge(s_h0t, g * GROUP + k + 1)
                    if k >= 2:
                        act.wait_ge(s_m1, g * GROUP + k - 1)
                    nc.scalar.copy(h0t[:, k % 2, :], bank[k % 2][:, 0:D]).then_inc(s_h0c, 1)
                deviation(0)
                for k in range(GROUP):
                    act.wait_ge(s_z1t, g * GROUP + k + 1)
                    if k >= 2:
                        act.wait_ge(s_m2, g * GROUP + k - 1)
                    for c in range(HC):
                        ins = nc.scalar.activation(act1t[:, k % 2, c * P:(c + 1) * P], bank[4 + k % 2][:, c * P:(c + 1) * P], ACT.Relu,
                                                   bias=beta1_col[:, c:c + 1], scale=g1_col[:, c:c + 1])
                    ins.then_inc(s_a1, 1)
                deviation(1)
                deviation(2)
                for k in range(GROUP):
                    act.wait_ge(s_yt, g * GROUP + k + 1)
                    if k >= 2:
                        act.wait_ge(s_lg, g * GROUP + k - 1)
                    nc.scalar.copy(yt[:, k % 2, :], bank[k % 2][:, 0:D]).then_inc(s_yc, 1)
                deviation(3)

            act.wait_ge(s_shift, 1)
            nc.scalar.activation(scores, work, ACT.Exp).then_inc(s_exp, 1)

            def slot_tile(j):
                for half in range(2):
                    act.wait_ge(s_ht, j * 2 + half + 1)
                    nc.scalar.activation(hid_t[:, half * BOUND:(half + 1) * BOUND], bank[half][:, :], ACT.Gelu).then_inc(s_ge, 1)

            with act.Fori(0, PAIRS) as i:
                for r in range(2):
                    slot_tile(i * 2 + r)
            for j in range(2 * PAIRS, SLOT_TILES):
                slot_tile(j)

            def stage(g, first):
                if not first:
                    act.wait_ge(s_sum, g * GROUP)
                nc.scalar.copy(slot_stage.rearrange("p (c k) -> p c k", c=ROUTED),
                               place[:, :].rearrange("p (c t) -> p c t", c=ROUTED)[:, :, bass.ds(g * GROUP, GROUP)]).then_inc(s_idx, 1)

            stage(0, True)
            with act.Fori(1, NG) as g:
                stage(g, False)

        @block.gpsimd
        def _(pool):
            nc.gpsimd.memset(zeros[:, :], 0.0).then_inc(s_zero, 1)
            pool.wait_ge(s_border_at, 1)
            for n, rows in enumerate((src_rows, dst_rows, weight_rows)):
                dst = border_rows[:, n * P:(n + 1) * P]
                pool.indirect_dma_start(dst[0:NT - 1, :] if n == 2 else dst[0:NT - 1, :].bitcast(I32), None, rows,
                                        bass.IndirectOffsetOnAxis(ap=border_at[0:NT - 1, :], axis=0)).then_inc(s_border_rows, 16)
            pool.wait_ge(s_xn_stored, 16 * NG)
            with pool.Fori(0, PASSES) as i:
                for k in range(RING):
                    if k % HALF == 0:
                        pool.wait_ge(s_staged, i * 2 + k // HALF + 1)
                    if k % 4 == 0:
                        pool.wait_ge(s_partial, i * RING + k + 4)
                        pool.sem_inc(s_wait, 1)
                    pool.indirect_dma_start(gathered[:, k, :], None, x_scratch,
                                            bass.IndirectOffsetOnAxis(ap=staged[:, k:k + 1], axis=0)).then_inc(s_gather[k], 16)

            pool.wait_ge(s_cleared, 16)
            with pool.Fori(0, NG) as g:
                for k in range(GROUP):
                    pool.wait_ge(s_row, g * GROUP + k + 1)
                    pool.sem_inc(s_wait, 1)
                    for c in range(ROUTED):
                        at = place_stage[:, c * GROUP + k:c * GROUP + k + 1]
                        pool.indirect_dma_start(slot_in, bass.IndirectOffsetOnAxis(ap=at, axis=0), row_stage[:, k, :], None).then_inc(s_sent[k], 16)

            for r in range(2):
                pool.wait_ge(s_y_stored[r], 16 * ((SLOT_TILES + 1 - r) // 2))

            def fetch(g, first):
                pool.wait_ge(s_idx, g + 1)
                for k in range(GROUP):
                    if not first:
                        pool.wait_ge(s_sum, g * GROUP + k + 1 - GROUP)
                    pool.sem_inc(s_wait, 1)
                    for c, dst in enumerate((first_y, second_y)):
                        at = slot_stage[:, c * GROUP + k:c * GROUP + k + 1]
                        pool.indirect_dma_start(dst[:, k, :], None, slot_out, bass.IndirectOffsetOnAxis(ap=at, axis=0)).then_inc(s_pair[k], 16)

            fetch(0, True)
            with pool.Fori(1, NG) as g:
                fetch(g, False)

        @block.tensor
        def _(pe):
            pe.sem_inc(s_partial, RING)
            pe.wait_ge(s_const, 16)
            pe.wait_ge(s_dstf, 1)
            CH = ET // 4
            for n in range(4):
                nc.tensor.matmul(bank[n][:, 0:CH], ones[0:1, :], dstf[0:1, n * CH:(n + 1) * CH], start=True, stop=True).then_inc(s_bcast, 1)
            pe.wait_ge(s_border_in, 1)
            for n in range(3):
                nc.tensor.transpose(bank[4 + n][:, 0:NT - 1], border[0:NT - 1, n * P:(n + 1) * P], ident[0:NT - 1, 0:NT - 1]).then_inc(s_border_t, 1)
            with pe.Fori(0, PASSES) as i:
                for k in range(RING):
                    pe.wait_ge(s_select, i * RING + k + 1)
                    pe.wait_ge(s_gather[k], i * 16 + 16)
                    pe.wait_ge(s_added, i * RING + k + 1)
                    nc.tensor.matmul(bank[k % SELS][:, 0:D], select[:, k % SELS, :], gathered[:, k, :], start=True, stop=True).then_inc(s_partial, 1)

            pe.wait_ge(s_param, 160)
            with pe.Fori(0, NG) as g:
                def turn(dst, src, chunks):
                    for c in range(chunks):
                        ins = nc.tensor.transpose(dst[:, c * P:(c + 1) * P], src[:, c * P:(c + 1) * P], ident)
                    return ins

                def product(dst, left, right, chunks, n):
                    for c in range(chunks):
                        ins = nc.tensor.matmul(dst, left[:, c * P:(c + 1) * P], right[:, c * n:(c + 1) * n], start=(c == 0), stop=(c == chunks - 1))
                    return ins

                for k in range(GROUP + 1):
                    if k < GROUP:
                        pe.wait_ge(s_h0, g * GROUP + k + 1)
                        if k >= 2:
                            pe.wait_ge(s_h0c, g * GROUP + k - 1)
                        turn(bank[k % 2], h0[:, k % 2, :], DC).then_inc(s_h0t, 1)
                    if k >= 1:
                        n = k - 1
                        pe.wait_ge(s_h0c, g * GROUP + n + 1)
                        if n >= 2:
                            pe.wait_ge(s_h1, g * GROUP + n - 1)
                        product(bank[2 + n % 2][:, 0:HID], h0t[:, n % 2, :], w1_sb, DC, HID).then_inc(s_m1, 1)
                for k in range(GROUP + 1):
                    if k < GROUP:
                        pe.wait_ge(s_z1, g * GROUP + k + 1)
                        if k >= 2:
                            pe.wait_ge(s_a1, g * GROUP + k - 1)
                        turn(bank[4 + k % 2], hidden[:, k * HID:(k + 1) * HID], HC).then_inc(s_z1t, 1)
                    if k >= 1:
                        n = k - 1
                        pe.wait_ge(s_a1, g * GROUP + n + 1)
                        if n >= 2:
                            pe.wait_ge(s_h2, g * GROUP + n - 1)
                        product(bank[6 + n % 2][:, 0:D], act1t[:, n % 2, :], w2_sb, HC, D).then_inc(s_m2, 1)
                for k in range(GROUP + 1):
                    if k < GROUP:
                        pe.wait_ge(s_y, g * GROUP + k + 1)
                        if k >= 2:
                            pe.wait_ge(s_yc, g * GROUP + k - 1)
                        turn(bank[k % 2], normed[:, k * D:(k + 1) * D], DC).then_inc(s_yt, 1)
                    if k >= 1:
                        n = k - 1
                        pe.wait_ge(s_yc, g * GROUP + n + 1)
                        if n >= 2:
                            pe.wait_ge(s_lt, g * GROUP + n - 1)
                        product(bank[2 + n % 2][:, 0:E], yt[:, n % 2, :], wr_sb, DC, E).then_inc(s_lg, 1)

            pe.wait_ge(s_both, 1)
            nc.tensor.matmul(bank[0][:, 0:NT * E], before, both, start=True, stop=True).then_inc(s_count, 1)
            nc.tensor.matmul(bank[1][:, 0:NT * E], ones, both, start=True, stop=True).then_inc(s_count, 1)

            pe.wait_ge(s_weights, 32 * E)

            def turn_rows(j, r, m):
                pe.wait_ge(s_xin[r], m * 16 + 16)
                for c in range(DC):
                    ins = nc.tensor.transpose(bank[4][:, c * P:(c + 1) * P], x_in[:, r, c * P:(c + 1) * P], ident)
                ins.then_inc(s_xt, 1)

            def up(j, r, e):
                pe.wait_ge(s_xs, j + 1)
                for half in range(2):
                    for c in range(DC):
                        w = w1_all[:, bass.ds(e * (DC * FF) + (c * FF + half * BOUND), BOUND)]
                        ins = nc.tensor.matmul(bank[2 + half][:, :], xt[:, r, c * P:(c + 1) * P], w, start=(c == 0), stop=(c == DC - 1))
                    ins.then_inc(s_f1, 1)

            def turn_hidden(j):
                for half in range(2):
                    pe.wait_ge(s_hb, j * 2 + half + 1)
                    for c in range(4):
                        at = half * BOUND + c * P
                        ins = nc.tensor.transpose(bank[half][:, c * P:(c + 1) * P], hid[:, at:at + P], ident)
                    ins.then_inc(s_ht, 1)

            def down(j, e):
                for c in range(FC):
                    if c % 4 == 0:
                        pe.wait_ge(s_ge, j * 2 + c // 4 + 1)
                    w = w2_all[:, bass.ds(e * (FC * D) + c * D, D)]
                    ins = nc.tensor.matmul(bank[5][:, 0:D], hid_t[:, c * P:(c + 1) * P], w, start=(c == 0), stop=(c == FC - 1))
                ins.then_inc(s_f2, 1)

            e0 = pe.value_load(tile_expert[0:1, 0:1], min_val=0, max_val=E - 1)
            turn_rows(0, 0, 0)
            up(0, 0, e0)
            turn_rows(1, 1, 0)

            def slot_tile(j, r, m, e, e_next):
                turn_hidden(j)
                if e_next is not None:
                    up(j + 1, 1 - r, e_next)
                if m is not None:
                    turn_rows(j + 2, r, m + 1)
                if m is None:
                    pe.wait_ge(s_ys, j)
                down(j, e)

            with pe.Fori(0, PAIRS) as i:
                _, e = nc.values_load_multi_w_load_instructions(tile_expert[0:1, bass.ds(i * 2, 4)], engines=[mybir.EngineType.PE], min_val=0, max_val=E - 1)
                for r in range(2):
                    slot_tile(i * 2 + r, r, i, e[r], e[r + 1])
            for j in range(2 * PAIRS, SLOT_TILES):
                e = [pe.value_load(tile_expert[0:1, n:n + 1], min_val=0, max_val=E - 1) for n in range(j, min(j + 2, SLOT_TILES))] + [None]
                slot_tile(j, j % 2, j // 2 if j + 2 < SLOT_TILES else None, e[0], e[1])

        @block.vector
        def _(dve):
            chain = Chain(dve, s_dve)
            GE = NT * E

            dve.wait_ge(s_edges, 48)
            dve.tensor_copy(dstf[:, 0:ET], dst_sb[:, 0:ET]).then_inc(s_dstf, 1)
            dve.memset(src_sb[:, ET:COLS], 0)
            dve.memset(agg[:, :], 0.0)
            CH = ET // 4
            for n in range(4):
                dve.wait_ge(s_bcast, n + 1)
                chain(dve.tensor_copy(lo_sb[:, n * CH:(n + 1) * CH], bank[n][:, 0:CH]))
            chain(dve.tensor_scalar(lo_sb[:, 0:ET], lo_sb[:, 0:ET], 7, None, ALU.arith_shift_right))
            lo_f = gathered[:, 0:7, :].rearrange("p r d -> p (r d)")[:, 0:ET]
            chain(dve.tensor_copy(lo_f, lo_sb[:, 0:ET]))
            chain(dve.scalar_tensor_tensor(out=rel_sb[:, 0:ET], in0=lo_f, scalar=-128.0, in1=dstf[:, 0:ET], op0=ALU.mult, op1=ALU.add))
            junk = gathered[:, 7:14, :].rearrange("p r d -> p (r d)")[0:NT - 1, 0:ET]
            cnt, base, dead = (border[0:NT - 1, 3 * P + n:3 * P + n + 1] for n in range(3))
            dve.wait_ge(s_const, 16)
            border_of = const[0:NT - 1, 4 * P:4 * P + 1]
            chain(dve.tensor_scalar(junk, lo_f[0:NT - 1, :], border_of, None, ALU.is_lt))
            chain(dve.tensor_reduce(cnt, junk, AX_X, ALU.add))
            dve.tensor_scalar(dead, cnt, 0.5, 65536.0, ALU.is_lt, ALU.mult)
            dve.tensor_scalar(border_at[0:NT - 1, :], cnt, -1.0, 0.0, ALU.add, ALU.max).then_inc(s_border_at, 1)
            dve.wait_ge(s_border_rows, 48)
            chain(dve.tensor_scalar(base, border_of, -128.0, None, ALU.mult))
            dve.tensor_copy(border[0:NT - 1, 0:P], border_rows[0:NT - 1, 0:P].bitcast(I32))
            dve.tensor_copy(border[0:NT - 1, 2 * P:3 * P], border_rows[0:NT - 1, 2 * P:3 * P])
            chain(dve.tensor_scalar(base, base, dead, None, ALU.add))
            dve.tensor_scalar(border[0:NT - 1, P:2 * P], border_rows[0:NT - 1, P:2 * P].bitcast(I32), base, None, ALU.add).then_inc(s_border_in, 1)
            dve.wait_ge(s_border_t, 3)
            dve.memset(rel_sb[:, STEPS:COLS], 0.0)
            dve.memset(wgt_sb[:, STEPS:COLS], 0.0)
            dve.tensor_scalar(lo_sb[:, ET:STEPS], iota[:, 0:NT - 1], 1.0, None, ALU.add)
            dve.tensor_copy(src_sb[:, ET:STEPS], bank[4][:, 0:NT - 1])
            dve.tensor_copy(rel_sb[:, ET:STEPS], bank[5][:, 0:NT - 1])
            chain(dve.tensor_copy(wgt_sb[:, ET:STEPS], bank[6][:, 0:NT - 1]))
            dve.sem_inc(s_added, SELS)
            dve.wait_ge(s_x, 16)
            for g in range(NG):
                for k in range(GROUP):
                    t = g * GROUP + k
                    ins = dve.bn_stats(stats[:, k * 6:k * 6 + 6], xn[:, t * D:(t + 1) * D])
                chain(ins)
                for k in range(GROUP):
                    ins = dve.bn_aggr(moments[:, 2 * k:2 * k + 2], stats[:, k * 6:k * 6 + 6])
                chain(ins)
                dve.tensor_scalar(moments[:, 1::2], moments[:, 1::2], LN_EPS, None, ALU.add).then_inc(s_sqrt_in, 1)
                dve.wait_ge(s_sqrt, g + 1)
                chain(dve.reciprocal(rstd[:, :], rstd[:, :]))
                for k in range(GROUP):
                    t = g * GROUP + k
                    ins = dve.tensor_scalar(xn[:, t * D:(t + 1) * D], xn[:, t * D:(t + 1) * D], moments[:, 2 * k:2 * k + 1],
                                            rstd[:, k:k + 1], ALU.subtract, ALU.mult)
                ins.then_inc(s_xn, 1)
            dve.sem_inc(s_plan, 1)

            def build_select(n, k):
                dve.tensor_scalar(select[:, k % SELS, :], iota, rel_sb[:, bass.ds(n, 1)], wgt_sb[:, bass.ds(n, 1)],
                                  ALU.is_equal, ALU.mult).then_inc(s_select, 1)

            for n in range(SELS - 1):
                build_select(n, n)
            with dve.Fori(0, PASSES) as i:
                _, tiles = nc.values_load_multi_w_load_instructions(lo_sb[0:1, bass.ds(i * RING, RING)], engines=[DVE], min_val=0, max_val=NT - 1,
                                                                    skip_runtime_bounds_check_because="node numbers are below the padded count")
                for k in range(RING):
                    dve.wait_ge(s_partial, i * RING + k + RING)
                    build_select(i * RING + k + SELS - 1, k + SELS - 1)
                    dve.wait_ge(s_added, i * RING + k + SELS)
                    dve.wait_ge(s_partial, i * RING + k + RING + 1)
                    rows = agg[:, bass.ds(tiles[k] * D, D)]
                    dve.tensor_tensor(rows, rows, bank[k % SELS][:, 0:D], ALU.add).then_inc(s_added, 1)
            dve.wait_ge(s_added, SELS + STEPS)

            dve.wait_ge(s_param, 160)
            with dve.Fori(0, NG) as g:
                chain.enter(g, PER_GROUP)
                base_tile = g * GROUP

                def settle():
                    dve.sem_inc(s_settle, 1)

                def node_stats(buf, width, n):
                    for k in range(GROUP):
                        ins = dve.bn_stats(g_stats[:, k * 6:k * 6 + 6], buf[:, k * width:(k + 1) * width])
                    finish_stats(ins, n)

                def finish_stats(ins, n):
                    chain(ins)
                    settle()
                    for k in range(GROUP):
                        ins = dve.bn_aggr(g_moments[:, 2 * k:2 * k + 2], g_stats[:, k * 6:k * 6 + 6])
                    chain(ins)
                    dve.tensor_scalar(g_moments[:, 1::2], g_moments[:, 1::2], LN_EPS, None, ALU.add).then_inc(s_var, 1)
                    dve.wait_ge(s_dev, g * 4 + n + 1)
                    chain(dve.reciprocal(g_rstd, g_rstd))

                def normalise(dst, src, k):
                    return dve.tensor_scalar(dst, src, g_moments[:, 2 * k:2 * k + 1], g_rstd[:, k:k + 1], ALU.subtract, ALU.mult)

                for k in range(GROUP + 1):
                    if k < GROUP:
                        if k >= 2:
                            dve.wait_ge(s_h0t, base_tile + k - 1)
                        cols = bass.ds((base_tile + k) * D, D)
                        dve.scalar_tensor_tensor(out=h0[:, k % 2, :], in0=xn[:, cols], scalar=eps_col, in1=agg[:, cols],
                                                 op0=ALU.mult, op1=ALU.add).then_inc(s_h0, 1)
                    if k >= 1:
                        n = k - 1
                        dve.wait_ge(s_m1, base_tile + n + 1)
                        dve.tensor_tensor(hidden[:, n * HID:(n + 1) * HID], bank[2 + n % 2][:, 0:HID], b1_row, ALU.add).then_inc(s_h1, 1)
                dve.wait_ge(s_h1, base_tile + GROUP)
                node_stats(hidden, HID, 0)
                for k in range(GROUP):
                    cols = slice(k * HID, (k + 1) * HID)
                    normalise(hidden[:, cols], hidden[:, cols], k).then_inc(s_z1, 1)
                for k in range(GROUP):
                    dve.wait_ge(s_m2, base_tile + k + 1)
                    dve.tensor_tensor(second[:, k * D:(k + 1) * D], bank[6 + k % 2][:, 0:D], b2_row, ALU.add).then_inc(s_h2, 1)
                dve.wait_ge(s_h2, base_tile + GROUP)
                node_stats(second, D, 1)
                for k in range(GROUP):
                    cols = slice(k * D, (k + 1) * D)
                    ins = normalise(second[:, cols], second[:, cols], k)
                chain(ins)

                def spread(row):
                    return row.rearrange("p (t d) -> p t d", t=1).to_broadcast([P, GROUP, D])

                chain(dve.tensor_tensor(tiled(second), tiled(second), spread(g2_row), ALU.mult))
                chain(dve.tensor_tensor(tiled(second), tiled(second), spread(beta2_row), ALU.add))
                dve.wait_ge(s_xg, g * 16 + 16)
                dve.scalar_tensor_tensor(out=x_group, in0=second, scalar=0.0, in1=x_group, op0=ALU.max, op1=ALU.add).then_inc(s_x1, 1)
                dve.wait_ge(s_x1, g + 1)
                node_stats(x_group, D, 2)
                for k in range(GROUP):
                    cols = slice(k * D, (k + 1) * D)
                    normalise(normed[:, cols], x_group[:, cols], k).then_inc(s_y, 1)
                dve.wait_ge(s_y, base_tile + GROUP)
                dve.sem_inc(s_xg_free, 1)
                for k in range(GROUP):
                    t = base_tile + k
                    dve.bn_stats(g_stats[:, k * 6:k * 6 + 6], normed[:, k * D:(k + 1) * D])
                    dve.wait_ge(s_lg, t + 1)
                    ins = dve.tensor_tensor(logits[:, bass.ds(t * E, E)], bank[2 + k % 2][:, 0:E], br_row, ALU.add)
                    ins.then_inc(s_lt, 1)
                finish_stats(dve.engine_nop(), 3)
                for k in range(GROUP):
                    t = base_tile + k
                    normalise(agg[:, bass.ds(t * D, D)], normed[:, k * D:(k + 1) * D], k)
            chain.leave(NG)
            dve.wait_ge(s_lt, NT)

            def te(view):
                return view.rearrange("p (t e) -> p t e", e=E)

            def over_experts(per_tok):
                return per_tok.rearrange("p (t e) -> p t e", e=1).to_broadcast([P, NT, E])

            def over_tokens(per_e):
                return per_e.rearrange("p (t e) -> p t e", t=1).to_broadcast([P, NT, E])

            top, total, key_top, denom = per_token
            chain(dve.tensor_reduce(top, te(logits[:, :]), AX_X, ALU.max))
            dve.tensor_tensor(te(work), te(logits[:, :]), over_experts(top), ALU.subtract).then_inc(s_shift, 1)
            rank = ahead[4]
            chain(dve.tensor_scalar(rank, iota[:, 0:E], -1.0, float(E), ALU.mult, ALU.add))
            dve.wait_ge(s_exp, 1)
            chain(dve.tensor_reduce(total, te(scores), AX_X, ALU.add))
            chain(dve.reciprocal(total, total))
            chain(dve.tensor_tensor(te(scores), te(scores), over_experts(total), ALU.mult))
            for c, onehot in enumerate((onehot0, onehot1)):
                weight = share[:, c * NT:(c + 1) * NT]
                chain(dve.tensor_reduce(weight, te(scores), AX_X, ALU.max))
                chain(dve.tensor_tensor(te(work), te(scores), over_experts(weight), ALU.is_equal))
                chain(dve.tensor_tensor(te(work), te(work), over_tokens(rank), ALU.mult))
                chain(dve.tensor_reduce(key_top, te(work), AX_X, ALU.max))
                chain(dve.tensor_tensor(te(onehot), te(work), over_experts(key_top), ALU.is_equal))
                if c == 0:
                    chain(dve.scalar_tensor_tensor(out=scores, in0=onehot, scalar=-2.0, in1=scores, op0=ALU.mult, op1=ALU.add))
            dve.tensor_tensor(both, onehot0, onehot1, ALU.add).then_inc(s_both, 1)
            chain(dve.tensor_tensor(denom, share[:, 0:NT], share[:, NT:2 * NT], ALU.add))
            chain(dve.reciprocal(denom, denom))
            for c in range(ROUTED):
                dve.tensor_tensor(share[:, c * NT:(c + 1) * NT], share[:, c * NT:(c + 1) * NT], denom, ALU.mult)
            dve.wait_ge(s_count, 2)
            chain(dve.tensor_copy(running, bank[1][:, 0:GE]))
            src_buf, dst_buf = running, other
            step = 1
            while step < NT:
                dve.tensor_copy(dst_buf[:, 0:step * E], src_buf[:, 0:step * E])
                chain(dve.tensor_tensor(dst_buf[:, step * E:GE], src_buf[:, step * E:GE], src_buf[:, 0:GE - step * E], ALU.add))
                src_buf, dst_buf = dst_buf, src_buf
                step *= 2
            tiles_f, tiles_i, end, end2 = ahead[:4]
            chain(dve.tensor_scalar(tiles_i.bitcast(I32), src_buf[:, GE - E:GE], float(P - 1), None, ALU.add))
            chain(dve.tensor_scalar(tiles_i.bitcast(I32), tiles_i.bitcast(I32), 7, None, ALU.arith_shift_right))
            chain(dve.tensor_copy(tiles_f, tiles_i.bitcast(I32)))
            a, b = tiles_f, end
            step = 1
            spare = [end, end2, tiles_i]
            for dst in spare:
                dve.tensor_copy(dst[:, 0:step], a[:, 0:step])
                chain(dve.tensor_tensor(dst[:, step:E], a[:, step:E], a[:, 0:E - step], ALU.add))
                a, step = dst, step * 2
            ends_e = a
            start_e = end
            chain(dve.tensor_tensor(start_e, ends_e, tiles_f, ALU.subtract))
            chain(dve.tensor_scalar(start_e, start_e, float(P), None, ALU.mult))
            chain(dve.tensor_tensor(dst_buf, src_buf, bank[1][:, 0:GE], ALU.subtract))
            chain(dve.tensor_tensor(dst_buf, dst_buf, bank[0][:, 0:GE], ALU.add))
            chain(dve.tensor_tensor(te(dst_buf), te(dst_buf), over_tokens(start_e), ALU.add))
            for c, onehot in enumerate((onehot0, onehot1)):
                chain(dve.tensor_tensor(work, onehot, dst_buf, ALU.mult))
                chain(dve.tensor_reduce(total, te(work), AX_X, ALU.add))
                chain(dve.tensor_copy(place[:, c * NT:(c + 1) * NT], total))
            j_of = iota.rearrange("p (j e) -> p j e", e=1).to_broadcast([P, P, E])
            chain(dve.tensor_tensor(ends.rearrange("p (j e) -> p j e", e=E), j_of,
                                    ends_e.rearrange("p (j e) -> p j e", j=1).to_broadcast([P, P, E]), ALU.is_ge))
            chain(dve.tensor_reduce(expert_f, ends.rearrange("p (j e) -> p j e", e=E), AX_X, ALU.add))
            dve.tensor_scalar(tile_expert[:, :], expert_f, float(E - 1), None, ALU.min).then_inc(s_routed, 1)
            dve.wait_ge(s_routed, 1)

            def stage_rows(g, first):
                for k in range(GROUP):
                    if not first:
                        dve.wait_ge(s_sent[k], g * (16 * ROUTED))
                    dve.tensor_copy(place_stage.rearrange("p (c k) -> p c k", c=ROUTED)[:, :, k:k + 1],
                                    place[:, :].rearrange("p (c t) -> p c t", c=ROUTED)[:, :, bass.ds(g * GROUP + k, 1)])
                    dve.tensor_copy(row_stage[:, k, :], agg[:, bass.ds((g * GROUP + k) * D, D)]).then_inc(s_row, 1)

            stage_rows(0, True)
            with dve.Fori(1, NG) as g:
                stage_rows(g, False)

            dve.wait_ge(s_weights, 32 * E)

            def scale_rows(j, r, e):
                dve.wait_ge(s_xt, j + 1)
                for c in range(DC):
                    at = bass.ds(e * DC + c, 1)
                    ins = dve.tensor_scalar(xt[:, r, c * P:(c + 1) * P], bank[4][:, c * P:(c + 1) * P], ln_g_col[:, at], ln_b_col[:, at], ALU.mult, ALU.add)
                ins.then_inc(s_xs, 1)

            def add_bias(j, r, m):
                dve.wait_ge(s_bias[r], m * 16 + 16)
                for half in range(2):
                    cols = slice(half * BOUND, (half + 1) * BOUND)
                    dve.wait_ge(s_f1, j * 2 + half + 1)
                    dve.tensor_tensor(hid[:, cols], bank[2 + half][:, :], bias[:, r, cols], ALU.add).then_inc(s_hb, 1)

            def take_output(j, r):
                dve.wait_ge(s_y_free, j + 1)
                dve.wait_ge(s_f2, j + 1)
                dve.tensor_tensor(y_sb[:, r, :], bank[5][:, 0:D], bias[:, r, FF:FF + D], ALU.add).then_inc(s_ys, 1)

            dve.sem_inc(s_y_free, 2)
            e0, e1 = (dve.value_load(tile_expert[0:1, n:n + 1], min_val=0, max_val=E - 1) for n in range(2))
            scale_rows(0, 0, e0)
            add_bias(0, 0, 0)
            scale_rows(1, 1, e1)

            def slot_tile(j, r, m, m_next, e_after):
                if m_next is not None:
                    add_bias(j + 1, 1 - r, m_next)
                if e_after is not None:
                    scale_rows(j + 2, r, e_after)
                take_output(j, r)

            with dve.Fori(0, PAIRS) as i:
                _, e = nc.values_load_multi_w_load_instructions(tile_expert[0:1, bass.ds(i * 2, 4)], engines=[DVE], min_val=0, max_val=E - 1)
                slot_tile(i * 2, 0, i, i, e[2])
                slot_tile(i * 2 + 1, 1, i, i + 1, e[3])
            for j in range(2 * PAIRS, SLOT_TILES):
                e_after = dve.value_load(tile_expert[0:1, j + 2:j + 3], min_val=0, max_val=E - 1) if j + 2 < SLOT_TILES else None
                slot_tile(j, j % 2, j // 2, (j + 1) // 2 if j + 1 < SLOT_TILES else None, e_after)

            with dve.Fori(0, NG) as g:
                dve.wait_ge(s_x1g, g * 16 + 16)
                for k in range(GROUP):
                    dve.wait_ge(s_pair[k], g * (16 * ROUTED) + 16 * ROUTED)
                    cols = slice(k * D, (k + 1) * D)
                    for c, y in enumerate((first_y, second_y)):
                        ins = dve.scalar_tensor_tensor(out=x1_group[:, cols], in0=y[:, k, :], scalar=share[:, bass.ds(g * GROUP + (c * NT + k), 1)],
                                                       in1=x1_group[:, cols], op0=ALU.mult, op1=ALU.add)
                        if c == 0:
                            ins.then_inc(s_half, 1)
                            dve.wait_ge(s_half, g * GROUP + k + 1)
                    ins.then_inc(s_sum, 1)


def kernel(**inputs):
    import numpy as np
    import concourse.bacc as bacc
    from concourse.bass_utils import run_bass_kernel_spmd as run

    inp = {k: np.asarray(v) for k, v in inputs.items()}
    N, D = inp["x"].shape
    nodes = -(-N // P) * P
    x = np.zeros((nodes, D), np.float32)
    x[:N] = inp["x"]
    edges = inp["src"].shape[0]
    tiles = -(-edges // (P * RING)) * RING

    def rows(a, fill):
        b = np.full((tiles * P,), fill, a.dtype)
        b[:edges] = a
        return b.reshape(tiles, P)

    src, dst, wgt = rows(inp["src"], 0), rows(inp["dst"], nodes - 1), rows(inp["edge_weight"], 0)
    k = np.arange(P, dtype=np.float32)
    consts = np.concatenate([np.eye(P), k[:, None] < k[None, :], np.tile(k, (P, 1)), np.ones((P, P)), k[:, None] + 1], axis=1).astype(np.float32)

    def tcol(a, w):
        return np.ascontiguousarray(a.reshape(-1, P).T)

    arrays = {
        "x": x, "src_rows": src, "dst_rows": dst, "weight_rows": wgt,
        "src_cols": np.ascontiguousarray(src.T), "dst_cols": np.ascontiguousarray(dst.T), "weight_cols": np.ascontiguousarray(wgt.T),
        "epsilon": inp["L0_gnn_epsilon"],
        "w1t": np.ascontiguousarray(inp["L0_gnn_w1"].T), "w2t": np.ascontiguousarray(inp["L0_gnn_w2"].T),
        "gnn_rows": np.concatenate([inp["L0_gnn_b1"], inp["L0_gnn_b2"], inp["L0_gnn_g2"], inp["L0_gnn_beta2"]])[None],
        "g1t": tcol(inp["L0_gnn_g1"], 4), "beta1t": tcol(inp["L0_gnn_beta1"], 4),
        "wr": inp["L0_ffn_Wr"], "br": inp["L0_ffn_br"][None],
        "ln_gt": tcol(inp["L0_ffn_ln_g"], 16), "ln_bt": tcol(inp["L0_ffn_ln_b"], 16),
        "expert_w1": inp["L0_ffn_W1"], "expert_w2": inp["L0_ffn_W2"],
        "expert_bias": np.concatenate([inp["L0_ffn_b1"], inp["L0_ffn_b2"]], axis=1),
        "consts": consts,
    }
    arrays = {n: np.ascontiguousarray(a) for n, a in arrays.items()}
    nc = bacc.Bacc("TRN2", target_bir_lowering=False, num_devices=1)
    args = [nc.dram_tensor(n, a.shape, mybir.dt.from_np(a.dtype), kind="ExternalInput").ap() for n, a in arrays.items()]
    out = nc.dram_tensor("out", (nodes, D), F32, kind="ExternalOutput").ap()
    gnn_moe(nc, *args, out)
    r = run(nc, [arrays], core_ids=[0])
    return r.results[0]["out"][:N]
```

```python
from contextlib import ExitStack

import concourse.bass as bass
from concourse import mybir

P = 128
F32 = mybir.dt.float32
I32 = mybir.dt.int32
ALU = mybir.AluOpType
ACT = mybir.ActivationFunctionType
AX_X = mybir.AxisListType.X
DVE = mybir.EngineType.DVE
LN_EPS = 1e-5
RING = 16
HALF = RING // 2
FREED = 4
SPAN = 2 * RING
SELS = 8
SUMS = 4
GROUP = 7
ROUTED = 2


class Chain:

    def __init__(self, eng, sem):
        self.eng, self.sem, self.n, self.loop = eng, sem, 0, None

    def value(self):
        if self.loop is None:
            return self.n
        i, start, per = self.loop
        return i * per + self.n

    def __call__(self, ins):
        self.n += 1
        ins.then_inc(self.sem, 1)
        self.eng.wait_ge(self.sem, self.value())

    def enter(self, i, per):
        self.loop = (i, self.n, per)

    def leave(self, passes):
        _, start, per = self.loop
        assert self.n - start == per, (self.n - start, per)
        self.n, self.loop = start + per * passes, None


def gnn_moe(nc, x, src_rows, dst_rows, weight_rows, src_cols, dst_cols, weight_cols, epsilon,
            w1t, w2t, gnn_rows, g1t, beta1t, wr, br, ln_gt, ln_bt, expert_w1, expert_w2,
            expert_bias, consts, out):
    NODES, D = x.shape
    NT = NODES // P
    NG = NT // GROUP
    ET = src_rows.shape[0]
    STEPS = ET + NT - 1
    PASSES = STEPS // RING
    BORDER_PASSES = (NT - 1) // RING
    SPANS = ET // SPAN
    REST_PASSES = (ET - SPANS * SPAN) // RING
    HID = w1t.shape[1]
    DC, HC = D // P, HID // P
    E, _, FF = expert_w1.shape
    FC = FF // P
    SLOT_TILES = (ROUTED * NODES + E * (P - 1)) // P
    BOUND = 512
    assert ET % RING == 0 and (NT - 1) % RING == 0 and NG * GROUP == NT and D == 256 and FF == 1024

    x_scratch = nc.dram_tensor("normed_nodes", (NODES, D), F32, kind="Internal").ap()
    x1_scratch = nc.dram_tensor("after_gnn", (NODES, D), F32, kind="Internal").ap()
    slot_in = nc.dram_tensor("slot_inputs", (SLOT_TILES * P, D), F32, kind="Internal").ap()
    slot_out = nc.dram_tensor("slot_outputs", (SLOT_TILES * P, D), F32, kind="Internal").ap()

    with ExitStack() as ctx:
        def sb(name, shape, dt=F32):
            return ctx.enter_context(nc.sbuf_tensor(name, shape, dt))

        def sem(name):
            return ctx.enter_context(nc.semaphore(name))

        region_a = sb("region_a", [P, E * DC * FF])
        region_b = sb("region_b", [P, E * FC * D])
        agg = sb("agg", [P, NT * D])
        const = sb("const", [P, 4 * P + 1])
        ident, before, iota, ones = (const[:, n * P:(n + 1) * P] for n in range(4))
        bank = [ctx.enter_context(nc.psum_tensor(f"bank{n}", [P, BOUND], F32)) for n in range(8)]

        xn = region_a[:, 0:NT * D]

        used = [0]

        def carve(n, dt=F32):
            at = used[0]
            used[0] += n
            assert used[0] <= E * FC * D
            view = region_b[:, at:at + n]
            return view if dt is F32 else view.bitcast(dt)

        w1_sb = sb("w1_sb", [P, DC * HID])
        w2_sb = sb("w2_sb", [P, HC * D])
        rows_sb = sb("rows_sb", [P, HID + 3 * D])
        b1_row, b2_row, g2_row, beta2_row = (rows_sb[:, a:b] for a, b in (
            (0, HID), (HID, HID + D), (HID + D, HID + 2 * D), (HID + 2 * D, HID + 3 * D)))
        small = sb("small", [P, 2 * HC + DC * E + E + 2 * E * DC + 1])
        at = 0
        views = []
        for width in (HC, HC, DC * E, E, E * DC, E * DC, 1):
            views.append(small[:, at:at + width])
            at += width
        g1_col, beta1_col, wr_sb, br_row, ln_g_col, ln_b_col, eps_col = views
        logits = sb("logits", [P, NT * E])
        share = sb("share", [P, ROUTED * NT])
        place = sb("place", [P, ROUTED * NT], I32)
        tile_expert = sb("tile_expert", [P, P], I32)
        zeros = sb("zeros", [P, D])
        ln_eps = sb("ln_eps", [P, 1])

        COLS = STEPS + RING
        src_sb, lo_sb = carve(COLS, I32), carve(COLS, I32)
        rel_sb, wgt_sb, dstf = carve(COLS), carve(COLS), carve(ET)
        dst_sb = carve(ET, I32)
        gathered = carve(RING * D).rearrange("p (r d) -> p r d", r=RING)
        select = carve(SELS * P).rearrange("p (r d) -> p r d", r=SELS)
        staged = carve(2 * RING, I32)
        border = carve(5 * P)
        border_rows = carve(3 * P)
        border_at = carve(1, I32)
        stats = carve(GROUP * 6)
        moments = carve(GROUP * 2)
        rstd = carve(GROUP)

        at = NT * D
        views = []
        for width in (HID, HID, D, D, D, D, D, D, 6, 2, 1):
            views.append(region_a[:, at:at + width])
            at += width
        hidden, act1t, h0, h0t, second, x_tile, normed, yt, n_stats, n_moments, n_rstd = views
        assert at <= E * DC * FF
        used[0] = 0
        scores, onehot0, onehot1, both, work, running, other = (carve(NT * E) for _ in range(7))
        per_token = [carve(NT) for _ in range(4)]
        ahead = [carve(E) for _ in range(5)]
        ends = carve(P * E)
        expert_f = carve(P)
        row_stage = carve(GROUP * D).rearrange("p (k d) -> p k d", k=GROUP)
        place_stage = carve(GROUP * ROUTED, I32)

        used_agg = [0]

        def carve_agg(n, dt=F32):
            at = used_agg[0]
            used_agg[0] += n
            assert used_agg[0] <= NT * D
            view = agg[:, at:at + n]
            return view if dt is F32 else view.bitcast(dt)

        x_in = carve_agg(2 * D).rearrange("p (r d) -> p r d", r=2)
        xt = carve_agg(2 * D).rearrange("p (r d) -> p r d", r=2)
        bias = carve_agg(2 * (FF + D)).rearrange("p (r d) -> p r d", r=2)
        hid, hid_t = carve_agg(FF), carve_agg(FF)
        y_sb = carve_agg(2 * D).rearrange("p (r d) -> p r d", r=2)
        first_y = carve_agg(GROUP * D).rearrange("p (k d) -> p k d", k=GROUP)
        second_y = carve_agg(GROUP * D).rearrange("p (k d) -> p k d", k=GROUP)
        x1_group = carve_agg(GROUP * D)
        slot_stage = carve_agg(GROUP * ROUTED, I32)
        w1_all = region_a
        w2_all = region_b

        s_const = sem("const_loaded")
        s_edges = sem("edges_loaded")
        s_x = sem("x_loaded")
        s_dve = sem("dve_step")
        s_sqrt_in = sem("variance_ready")
        s_sqrt = sem("deviation_ready")
        s_xn = sem("normed_ready")
        s_xn_stored = sem("normed_stored")
        s_dstf = sem("dst_float_ready")
        s_bcast = sem("first_dst_spread")
        s_border_at = sem("border_tile_known")
        s_border_rows = sem("border_rows_gathered")
        s_border_in = sem("border_rows_ready")
        s_border_t = sem("border_rows_turned")
        s_plan = sem("plan_ready")
        s_staged = sem("indices_staged")
        s_gather = [sem(f"gathered{n}") for n in range(RING)]
        s_select = sem("selection_ready")
        s_partial = sem("partial_sum_ready")
        s_added = sem("partial_sum_added")
        s_claimed = sem("slots_claimed")

        s_param = sem("parameters_loaded")
        s_zero = sem("zero_tile_ready")
        s_cleared = sem("slots_cleared")
        s_xg = sem("x_tile_loaded")
        s_x1 = sem("x1_ready")
        s_node = sem("node_layer_step")
        s_x1_stored = sem("x1_stored")
        s_h0, s_h0t, s_h0c, s_m1, s_h1 = (sem(n) for n in ("h0_ready", "h0_turned", "h0_copied", "product1_ready", "product1_taken"))
        s_var, s_dev = sem("group_variance_ready"), sem("group_deviation_ready")
        s_z1, s_z1t, s_a1, s_m2, s_h2 = (sem(n) for n in ("z1_ready", "z1_turned", "act1_ready", "product2_ready", "product2_taken"))
        s_y, s_yt, s_yc, s_lg, s_lt = (sem(n) for n in ("y_ready", "y_turned", "y_copied", "logits_ready", "logits_taken"))
        s_shift, s_exp, s_both, s_count, s_routed = (sem(n) for n in ("shifted_ready", "exponentials_ready", "choice_ready", "counts_ready", "routing_ready"))
        s_row = sem("row_tile_staged")
        s_sent = [sem(f"rows_sent{k}") for k in range(GROUP)]
        s_wait = sem("pool_waited")
        s_settle = sem("dve_settled")
        s_weights = sem("expert_weights_loaded")
        s_xin = [sem(f"slot_rows_loaded{r}") for r in range(2)]
        s_bias = [sem(f"bias_loaded{r}") for r in range(2)]
        s_xt, s_xs, s_f1, s_hb, s_ht, s_ge, s_f2, s_ys = (sem(n) for n in (
            "slot_rows_turned", "slot_rows_scaled", "up_ready", "up_biased", "up_turned", "gelu_ready", "down_ready", "down_biased"))
        s_y_free = sem("slot_output_stored_and_free")
        s_y_stored = [sem(f"slot_output_stored{r}") for r in range(2)]
        s_idx = sem("slots_staged")
        s_pair = [sem(f"pair_gathered{k}") for k in range(GROUP)]
        s_x1g = sem("x1_group_loaded")
        s_half = sem("first_output_added")
        s_sum = sem("sum_ready")
        s_out = sem("out_stored")

        block = ctx.enter_context(nc.Block())

        def group_rows(dram, g):
            return dram[bass.ds(g * (GROUP * P), GROUP * P), :].rearrange("(t p) d -> p t d", p=P)

        def tiled(view):
            return view.rearrange("p (t d) -> p t d", d=D)

        PER_TILE = 13
        LOOKED = 2
        PAIRS = (SLOT_TILES - LOOKED) // 2

        @block.sync
        def _(sp):
            for src, dst in ((dst_cols, dst_sb), (src_cols, src_sb[:, NT - 1:STEPS]), (weight_cols, wgt_sb[:, NT - 1:STEPS])):
                sp.dma_start(dst, src).then_inc(s_edges, 16)
            sp.dma_start(const[:, :], consts).then_inc(s_const, 16)
            sp.dma_start(tiled(xn), x.rearrange("(t p) d -> p t d", p=P)).then_inc(s_x, 16)
            for g in range(NG):
                sp.wait_ge(s_xn, g + 1)
                sp.dma_start(group_rows(x_scratch, g), tiled(xn[:, g * GROUP * D:(g + 1) * GROUP * D])).then_inc(s_xn_stored, 16)
            params = ((w1_sb[:, :].rearrange("p (c n) -> p c n", c=DC), w1t.rearrange("(c p) n -> p c n", p=P)),
                      (w2_sb[:, :].rearrange("p (c n) -> p c n", c=HC), w2t.rearrange("(c p) n -> p c n", p=P)),
                      (rows_sb[:, :], gnn_rows.to_broadcast([P, HID + 3 * D])), (g1_col, g1t), (beta1_col, beta1t),
                      (wr_sb.rearrange("p (c n) -> p c n", c=DC), wr.rearrange("(c p) n -> p c n", p=P)),
                      (br_row, br.to_broadcast([P, E])), (ln_g_col, ln_gt), (ln_b_col, ln_bt),
                      (eps_col, epsilon.to_broadcast([P, 1])))
            for dst, src in params:
                sp.dma_start(dst, src).then_inc(s_param, 16)
            sp.wait_ge(s_zero, 2)
            sp.dma_start(slot_in.rearrange("(t p) d -> p t d", p=P),
                         zeros[:, :].rearrange("p (t d) -> p t d", t=1).to_broadcast([P, SLOT_TILES, D])).then_inc(s_cleared, 16)

            def node_rows(dram, t):
                return dram[bass.ds(t * P, P), :]

            sp.dma_start(x_tile, node_rows(x, 0)).then_inc(s_xg, 16)
            with sp.Fori(0, NT - 1) as t:
                sp.wait_ge(s_x1, t + 1)
                sp.dma_start(node_rows(x1_scratch, t), x_tile).then_inc(s_x1_stored, 16)
                sp.wait_ge(s_x1_stored, t * 16 + 16)
                sp.wait_ge(s_y, t + 1)
                sp.dma_start(x_tile, node_rows(x, t + 1)).then_inc(s_xg, 16)
            sp.wait_ge(s_x1, NT)
            sp.dma_start(node_rows(x1_scratch, NT - 1), x_tile).then_inc(s_x1_stored, 16)

            sp.wait_ge(s_routed, 1)
            for e in range(E):
                sp.dma_start(w1_all[:, e * DC * FF:(e + 1) * DC * FF].rearrange("p (c n) -> p c n", c=DC),
                             expert_w1[e].rearrange("(c p) n -> p c n", p=P)).then_inc(s_weights, 16)
            for k in range(GROUP):
                sp.wait_ge(s_sent[k], 16 * ROUTED * NG)
            sp.wait_ge(s_x1_stored, 16 * NT)
            for e in range(E):
                sp.dma_start(w2_all[:, e * FC * D:(e + 1) * FC * D].rearrange("p (c n) -> p c n", c=FC),
                             expert_w2[e].rearrange("(c p) n -> p c n", p=P)).then_inc(s_weights, 16)

            def load_rows(j, r):
                sp.dma_start(x_in[:, r, :], slot_in[bass.ds(j * P, P), :]).then_inc(s_xin[r], 16)

            def load_bias(j, r):
                e = sp.value_load(tile_expert[0:1, bass.ds(j, 1)], min_val=0, max_val=E - 1)
                sp.dma_start(bias[:, r, :], expert_bias[bass.ds(e, 1), :].to_broadcast([P, FF + D])).then_inc(s_bias[r], 16)

            AHEAD = 2 * LOOKED

            def slot_tile(j, r, m):
                load_more = not isinstance(j, int) or j + AHEAD < SLOT_TILES
                if load_more:
                    sp.wait_ge(s_xt, j + LOOKED + 1)
                    load_rows(j + AHEAD, r)
                sp.wait_ge(s_ys, j + 2)
                sp.dma_start(slot_out[bass.ds(j * P, P), :], y_sb[:, r, :]).then_inc(s_y_stored[r], 16)
                if load_more or j + LOOKED < SLOT_TILES:
                    load_bias(j + LOOKED, r)
                sp.wait_ge(s_y_stored[r], m * 16 + 16)
                sp.sem_inc(s_y_free, 1)

            for j in range(LOOKED):
                load_rows(j, j)
                load_bias(j, j)
            for j in range(LOOKED):
                sp.wait_ge(s_xt, j + 1)
                load_rows(j + LOOKED, j)
            SP_PAIRS = (SLOT_TILES - AHEAD) // 2
            with sp.Fori(0, SP_PAIRS) as i:
                for r in range(2):
                    slot_tile(i * 2 + r, r, i)
            for j in range(2 * SP_PAIRS, SLOT_TILES):
                slot_tile(j, j % 2, j // 2)

            def load_x1(g):
                sp.dma_start(tiled(x1_group), group_rows(x1_scratch, g)).then_inc(s_x1g, 16)

            load_x1(0)
            with sp.Fori(0, NG - 1) as g:
                sp.wait_ge(s_sum, (g + 1) * GROUP)
                sp.dma_start(group_rows(out, g), tiled(x1_group)).then_inc(s_out, 16)
                sp.wait_ge(s_out, (g + 1) * 16)
                load_x1(g + 1)
            sp.wait_ge(s_sum, NT)
            sp.dma_start(group_rows(out, NG - 1), tiled(x1_group)).then_inc(s_out, 16)
            sp.wait_ge(s_out, 16 * NG)

        @block.scalar
        def _(act):
            for g in range(NG):
                act.wait_ge(s_sqrt_in, g + 1)
                nc.scalar.activation(rstd[:, :], moments[:, 1::2], ACT.Sqrt).then_inc(s_sqrt, 1)
            act.wait_ge(s_param, 160)
            act.wait_ge(s_zero, 2)

            def deviation(t, n):
                act.wait_ge(s_var, t * 4 + n + 1)
                nc.scalar.activation(n_rstd, n_moments[:, 1:2], ACT.Sqrt, bias=ln_eps[:, :]).then_inc(s_dev, 1)

            def node_tile(t):
                act.wait_ge(s_h0t, t + 1)
                nc.scalar.copy(h0t, bank[4][:, 0:D]).then_inc(s_h0c, 1)
                deviation(t, 0)
                act.wait_ge(s_z1t, t + 1)
                for c in range(HC):
                    ins = nc.scalar.activation(act1t[:, c * P:(c + 1) * P], bank[6][:, c * P:(c + 1) * P], ACT.Relu,
                                               bias=beta1_col[:, c:c + 1], scale=g1_col[:, c:c + 1])
                ins.then_inc(s_a1, 1)
                deviation(t, 1)
                deviation(t, 2)
                act.wait_ge(s_yt, t + 1)
                nc.scalar.copy(yt, bank[4][:, 0:D]).then_inc(s_yc, 1)
                deviation(t, 3)

            act.wait_ge(s_plan, 1)
            with act.Fori(0, NT) as t:
                node_tile(t)

            act.wait_ge(s_shift, 1)
            nc.scalar.activation(scores, work, ACT.Exp).then_inc(s_exp, 1)

            def slot_tile(j):
                for half in range(2):
                    act.wait_ge(s_ht, j * 2 + half + 1)
                    nc.scalar.activation(hid_t[:, half * BOUND:(half + 1) * BOUND], bank[half][:, :], ACT.Gelu).then_inc(s_ge, 1)

            with act.Fori(0, PAIRS) as i:
                for r in range(2):
                    slot_tile(i * 2 + r)
            for j in range(2 * PAIRS, SLOT_TILES):
                slot_tile(j)

            def stage(g, first):
                if not first:
                    act.wait_ge(s_sum, g * GROUP)
                nc.scalar.copy(slot_stage.rearrange("p (c k) -> p c k", c=ROUTED),
                               place[:, :].rearrange("p (c t) -> p c t", c=ROUTED)[:, :, bass.ds(g * GROUP, GROUP)]).then_inc(s_idx, 1)

            stage(0, True)
            with act.Fori(1, NG) as g:
                stage(g, False)

        @block.gpsimd
        def _(pool):
            nc.gpsimd.memset(zeros[:, :], 0.0).then_inc(s_zero, 1)
            nc.gpsimd.memset(ln_eps[:, :], LN_EPS).then_inc(s_zero, 1)
            pool.wait_ge(s_border_at, 1)
            for n, rows in enumerate((src_rows, dst_rows, weight_rows)):
                dst = border_rows[:, n * P:(n + 1) * P]
                pool.indirect_dma_start(dst[0:NT - 1, :] if n == 2 else dst[0:NT - 1, :].bitcast(I32), None, rows,
                                        bass.IndirectOffsetOnAxis(ap=border_at[0:NT - 1, :], axis=0)).then_inc(s_border_rows, 16)
            pool.wait_ge(s_xn_stored, 16 * NG)
            pool.wait_ge(s_plan, 1)
            with pool.Fori(0, PASSES // 2) as pair:
                for half in range(4):
                    i, first = pair * 2 + half // 2, half % 2 * HALF
                    now = staged[:, half * HALF:(half + 1) * HALF]
                    nc.gpsimd.tensor_copy(now, src_sb[:, bass.ds(i * RING + first, HALF)]).then_inc(s_staged, 1)
                    pool.wait_ge(s_staged, pair * 4 + half + 1)
                    for k in range(first, first + HALF):
                        if k % FREED == 0:
                            pool.wait_ge(s_partial, i * RING + k + FREED)
                            pool.sem_inc(s_wait, 1)
                        pool.indirect_dma_start(gathered[:, k, :], None, x_scratch,
                                                bass.IndirectOffsetOnAxis(ap=now[:, k - first:k - first + 1], axis=0)).then_inc(s_gather[k], 16)

            pool.wait_ge(s_cleared, 16)
            with pool.Fori(0, NG) as g:
                for k in range(GROUP):
                    pool.wait_ge(s_row, g * GROUP + k + 1)
                    pool.sem_inc(s_wait, 1)
                    for c in range(ROUTED):
                        at = place_stage[:, c * GROUP + k:c * GROUP + k + 1]
                        pool.indirect_dma_start(slot_in, bass.IndirectOffsetOnAxis(ap=at, axis=0), row_stage[:, k, :], None).then_inc(s_sent[k], 16)

            for r in range(2):
                pool.wait_ge(s_y_stored[r], 16 * ((SLOT_TILES + 1 - r) // 2))

            def fetch(g, first):
                pool.wait_ge(s_idx, g + 1)
                for k in range(GROUP):
                    if not first:
                        pool.wait_ge(s_sum, g * GROUP + k + 1 - GROUP)
                    pool.sem_inc(s_wait, 1)
                    for c, dst in enumerate((first_y, second_y)):
                        at = slot_stage[:, c * GROUP + k:c * GROUP + k + 1]
                        pool.indirect_dma_start(dst[:, k, :], None, slot_out, bass.IndirectOffsetOnAxis(ap=at, axis=0)).then_inc(s_pair[k], 16)

            fetch(0, True)
            with pool.Fori(1, NG) as g:
                fetch(g, False)

        @block.tensor
        def _(pe):
            pe.sem_inc(s_partial, RING)
            pe.wait_ge(s_const, 16)
            pe.wait_ge(s_dstf, 1)
            CH = ET // 4
            for n in range(4):
                nc.tensor.matmul(bank[n][:, 0:CH], ones[0:1, :], dstf[0:1, n * CH:(n + 1) * CH], start=True, stop=True).then_inc(s_bcast, 1)
            pe.wait_ge(s_border_in, 1)
            for n in range(3):
                nc.tensor.transpose(bank[4 + n][:, 0:NT - 1], border[0:NT - 1, n * P:(n + 1) * P], ident[0:NT - 1, 0:NT - 1]).then_inc(s_border_t, 1)
            def turn(dst, src, chunks):
                for c in range(chunks):
                    ins = nc.tensor.transpose(dst[:, c * P:(c + 1) * P], src[:, c * P:(c + 1) * P], ident)
                return ins

            def product(dst, left, right, chunks, n):
                for c in range(chunks):
                    ins = nc.tensor.matmul(dst, left[:, c * P:(c + 1) * P], right[:, c * n:(c + 1) * n], start=(c == 0), stop=(c == chunks - 1))
                return ins

            def sum_step(i, k):
                pe.wait_ge(s_select, i * RING + k + 1)
                pe.wait_ge(s_gather[k], i * 16 + 16)
                pe.wait_ge(s_added, i * RING + k + 1)
                nc.tensor.matmul(bank[k % SUMS][:, 0:D], select[:, k % SELS, :], gathered[:, k, :], start=True, stop=True).then_inc(s_partial, 1)

            def node_tile(t):
                yield 4
                pe.wait_ge(s_h0, t + 1)
                turn(bank[4], h0, DC).then_inc(s_h0t, 1)
                for c in range(DC):
                    yield 2 - c
                    if c == 0:
                        pe.wait_ge(s_h0c, t + 1)
                    ins = nc.tensor.matmul(bank[5][:, 0:HID], h0t[:, c * P:(c + 1) * P], w1_sb[:, c * HID:(c + 1) * HID], start=(c == 0), stop=(c == DC - 1))
                ins.then_inc(s_m1, 1)
                yield 5
                pe.wait_ge(s_z1, t + 1)
                turn(bank[6], hidden, HC).then_inc(s_z1t, 1)
                yield 2
                for c in range(HC):
                    yield 1
                    if c == 0:
                        pe.wait_ge(s_a1, t + 1)
                    ins = nc.tensor.matmul(bank[7][:, 0:D], act1t[:, c * P:(c + 1) * P], w2_sb[:, c * D:(c + 1) * D], start=(c == 0), stop=(c == HC - 1))
                ins.then_inc(s_m2, 1)
                yield 9
                pe.wait_ge(s_y, t + 1)
                turn(bank[4], normed, DC).then_inc(s_yt, 1)
                yield 2
                pe.wait_ge(s_yc, t + 1)
                for c in range(DC):
                    ins = nc.tensor.matmul(bank[5][:, 0:E], yt[:, c * P:(c + 1) * P], wr_sb[:, c * E:(c + 1) * E], start=(c == 0), stop=(c == DC - 1))
                ins.then_inc(s_lg, 1)

            pe.wait_ge(s_param, 160)
            with pe.Fori(0, BORDER_PASSES) as i:
                for k in range(RING):
                    sum_step(i, k)
            tiles_done = pe.alloc_register("tiles_done_pe")
            pe.reg_mov(tiles_done, 0)
            with pe.Fori(0, SPANS) as i:
                complete = pe.value_load(lo_sb[0:1, bass.ds(i * SPAN + (NT - 1), 1)], min_val=0, max_val=NT)
                with pe.If_lt(tiles_done, complete):
                    part = node_tile(pe.snap(tiles_done, min_val=0, max_val=NT - 1))
                    to_take = next(part)
                    for k in range(SPAN):
                        sum_step(i * 2 + (BORDER_PASSES + k // RING), k % RING)
                        to_take -= 1
                        while to_take == 0:
                            to_take = next(part, None)
                            if to_take is None:
                                to_take = SPAN
                    for _ in part:
                        pass
                    pe.reg_add(tiles_done, tiles_done, 1)
                with pe.Else():
                    for k in range(SPAN):
                        sum_step(i * 2 + (BORDER_PASSES + k // RING), k % RING)
            with pe.Fori(PASSES - REST_PASSES, PASSES) as i:
                for k in range(RING):
                    sum_step(i, k)
            with pe.Fori(0, NT):
                with pe.If_lt(tiles_done, NT):
                    for _ in node_tile(pe.snap(tiles_done, min_val=0, max_val=NT - 1)):
                        pass
                    pe.reg_add(tiles_done, tiles_done, 1)

            pe.wait_ge(s_both, 1)
            nc.tensor.matmul(bank[0][:, 0:NT * E], before, both, start=True, stop=True).then_inc(s_count, 1)
            nc.tensor.matmul(bank[1][:, 0:NT * E], ones, both, start=True, stop=True).then_inc(s_count, 1)

            pe.wait_ge(s_weights, 32 * E)

            def turn_rows(j, r, m):
                pe.wait_ge(s_xin[r], m * 16 + 16)
                for c in range(DC):
                    ins = nc.tensor.transpose(bank[4][:, c * P:(c + 1) * P], x_in[:, r, c * P:(c + 1) * P], ident)
                ins.then_inc(s_xt, 1)

            def up(j, r, e):
                pe.wait_ge(s_xs, j + 1)
                for half in range(2):
                    for c in range(DC):
                        w = w1_all[:, bass.ds(e * (DC * FF) + (c * FF + half * BOUND), BOUND)]
                        ins = nc.tensor.matmul(bank[2 + half][:, :], xt[:, r, c * P:(c + 1) * P], w, start=(c == 0), stop=(c == DC - 1))
                    ins.then_inc(s_f1, 1)

            def turn_hidden(j):
                for half in range(2):
                    pe.wait_ge(s_hb, j * 2 + half + 1)
                    for c in range(4):
                        at = half * BOUND + c * P
                        ins = nc.tensor.transpose(bank[half][:, c * P:(c + 1) * P], hid[:, at:at + P], ident)
                    ins.then_inc(s_ht, 1)

            def down(j, e):
                for c in range(FC):
                    if c % 4 == 0:
                        pe.wait_ge(s_ge, j * 2 + c // 4 + 1)
                    w = w2_all[:, bass.ds(e * (FC * D) + c * D, D)]
                    ins = nc.tensor.matmul(bank[5][:, 0:D], hid_t[:, c * P:(c + 1) * P], w, start=(c == 0), stop=(c == FC - 1))
                ins.then_inc(s_f2, 1)

            e0 = pe.value_load(tile_expert[0:1, 0:1], min_val=0, max_val=E - 1)
            turn_rows(0, 0, 0)
            up(0, 0, e0)
            turn_rows(1, 1, 0)

            def slot_tile(j, r, m, e, e_next):
                turn_hidden(j)
                if e_next is not None:
                    up(j + 1, 1 - r, e_next)
                if m is not None:
                    turn_rows(j + 2, r, m + 1)
                pe.wait_ge(s_ys, j + 1)
                down(j, e)

            with pe.Fori(0, PAIRS) as i:
                _, e = nc.values_load_multi_w_load_instructions(tile_expert[0:1, bass.ds(i * 2, 4)], engines=[mybir.EngineType.PE], min_val=0, max_val=E - 1)
                for r in range(2):
                    slot_tile(i * 2 + r, r, i, e[r], e[r + 1])
            for j in range(2 * PAIRS, SLOT_TILES):
                e = [pe.value_load(tile_expert[0:1, n:n + 1], min_val=0, max_val=E - 1) for n in range(j, min(j + 2, SLOT_TILES))] + [None]
                slot_tile(j, j % 2, j // 2 if j + 2 < SLOT_TILES else None, e[0], e[1])

        @block.vector
        def _(dve):
            chain = Chain(dve, s_dve)
            GE = NT * E

            dve.wait_ge(s_edges, 48)
            dve.tensor_copy(dstf, dst_sb).then_inc(s_dstf, 1)
            dve.memset(src_sb[:, STEPS:COLS], 0)
            dve.memset(agg[:, :], 0.0)
            CH = ET // 4
            for n in range(4):
                dve.wait_ge(s_bcast, n + 1)
                chain(dve.tensor_copy(lo_sb[:, NT - 1 + n * CH:NT - 1 + (n + 1) * CH], bank[n][:, 0:CH]))
            chain(dve.tensor_scalar(lo_sb[:, NT - 1:STEPS], lo_sb[:, NT - 1:STEPS], 7, None, ALU.arith_shift_right))
            lo_f = gathered[:, 0:7, :].rearrange("p r d -> p (r d)")[:, 0:ET]
            chain(dve.tensor_copy(lo_f, lo_sb[:, NT - 1:STEPS]))
            chain(dve.scalar_tensor_tensor(out=rel_sb[:, NT - 1:STEPS], in0=lo_f, scalar=-128.0, in1=dstf, op0=ALU.mult, op1=ALU.add))
            junk = gathered[:, 7:14, :].rearrange("p r d -> p (r d)")[0:NT - 1, 0:ET]
            cnt, base, dead = (border[0:NT - 1, 3 * P + n:3 * P + n + 1] for n in range(3))
            dve.wait_ge(s_const, 16)
            border_of = const[0:NT - 1, 4 * P:4 * P + 1]
            chain(dve.tensor_scalar(junk, lo_f[0:NT - 1, :], border_of, None, ALU.is_lt))
            chain(dve.tensor_reduce(cnt, junk, AX_X, ALU.add))
            dve.tensor_scalar(dead, cnt, 0.5, 65536.0, ALU.is_lt, ALU.mult)
            dve.tensor_scalar(border_at[0:NT - 1, :], cnt, -1.0, 0.0, ALU.add, ALU.max).then_inc(s_border_at, 1)
            dve.wait_ge(s_border_rows, 48)
            chain(dve.tensor_scalar(base, border_of, -128.0, None, ALU.mult))
            dve.tensor_copy(border[0:NT - 1, 0:P], border_rows[0:NT - 1, 0:P].bitcast(I32))
            dve.tensor_copy(border[0:NT - 1, 2 * P:3 * P], border_rows[0:NT - 1, 2 * P:3 * P])
            chain(dve.tensor_scalar(base, base, dead, None, ALU.add))
            dve.tensor_scalar(border[0:NT - 1, P:2 * P], border_rows[0:NT - 1, P:2 * P].bitcast(I32), base, None, ALU.add).then_inc(s_border_in, 1)
            dve.wait_ge(s_border_t, 3)
            dve.memset(rel_sb[:, STEPS:COLS], 0.0)
            dve.memset(wgt_sb[:, STEPS:COLS], 0.0)
            dve.tensor_scalar(lo_sb[:, 0:NT - 1], iota[:, 0:NT - 1], 1.0, None, ALU.add)
            dve.tensor_copy(src_sb[:, 0:NT - 1], bank[4][:, 0:NT - 1])
            dve.tensor_copy(rel_sb[:, 0:NT - 1], bank[5][:, 0:NT - 1])
            chain(dve.tensor_copy(wgt_sb[:, 0:NT - 1], bank[6][:, 0:NT - 1]))
            dve.sem_inc(s_added, SUMS)
            dve.wait_ge(s_x, 16)
            for g in range(NG):
                for k in range(GROUP):
                    t = g * GROUP + k
                    ins = dve.bn_stats(stats[:, k * 6:k * 6 + 6], xn[:, t * D:(t + 1) * D])
                chain(ins)
                for k in range(GROUP):
                    ins = dve.bn_aggr(moments[:, 2 * k:2 * k + 2], stats[:, k * 6:k * 6 + 6])
                chain(ins)
                dve.tensor_scalar(moments[:, 1::2], moments[:, 1::2], LN_EPS, None, ALU.add).then_inc(s_sqrt_in, 1)
                dve.wait_ge(s_sqrt, g + 1)
                chain(dve.reciprocal(rstd[:, :], rstd[:, :]))
                for k in range(GROUP):
                    t = g * GROUP + k
                    ins = dve.tensor_scalar(xn[:, t * D:(t + 1) * D], xn[:, t * D:(t + 1) * D], moments[:, 2 * k:2 * k + 1],
                                            rstd[:, k:k + 1], ALU.subtract, ALU.mult)
                ins.then_inc(s_xn, 1)
            dve.sem_inc(s_plan, 1)

            def build_select(n, k):
                dve.tensor_scalar(select[:, k % SELS, :], iota, rel_sb[:, bass.ds(n, 1)], wgt_sb[:, bass.ds(n, 1)],
                                  ALU.is_equal, ALU.mult).then_inc(s_select, 1)

            for n in range(SELS - 1):
                build_select(n, n)
            def sum_step(i, k, tile):
                dve.wait_ge(s_partial, i * RING + k + RING)
                build_select(i * RING + k + SELS - 1, k + SELS - 1)
                dve.wait_ge(s_added, i * RING + k + SUMS)
                dve.wait_ge(s_partial, i * RING + k + RING + 1)
                rows = agg[:, bass.ds(tile * D, D)]
                dve.tensor_tensor(rows, rows, bank[k % SUMS][:, 0:D], ALU.add).then_inc(s_added, 1)

            def node_tile(t):
                own = Chain(dve, s_node)
                own.enter(t, PER_TILE)

                def moments_of(view):
                    own(dve.bn_stats(n_stats, view))
                    dve.sem_inc(s_settle, 1)
                    dve.bn_aggr(n_moments, n_stats).then_inc(s_var, 1)

                def normalise(dst, src, n):
                    dve.wait_ge(s_dev, t * 4 + n + 1)
                    own(dve.reciprocal(n_rstd, n_rstd))
                    return dve.tensor_scalar(dst, src, n_moments[:, 0:1], n_rstd, ALU.subtract, ALU.mult)

                yield 1
                cols = bass.ds(t * D, D)
                dve.scalar_tensor_tensor(out=h0, in0=xn[:, cols], scalar=eps_col, in1=agg[:, cols], op0=ALU.mult, op1=ALU.add).then_inc(s_h0, 1)
                yield 5
                dve.wait_ge(s_m1, t + 1)
                own(dve.tensor_tensor(hidden, bank[5][:, 0:HID], b1_row, ALU.add))
                yield 1
                moments_of(hidden)
                yield 2
                normalise(hidden, hidden, 0).then_inc(s_z1, 1)
                yield 8
                dve.wait_ge(s_m2, t + 1)
                own(dve.tensor_tensor(second, bank[7][:, 0:D], b2_row, ALU.add))
                moments_of(second)
                yield 2
                own(normalise(second, second, 1))
                own(dve.tensor_tensor(second, second, g2_row, ALU.mult))
                yield 1
                own(dve.tensor_tensor(second, second, beta2_row, ALU.add))
                dve.wait_ge(s_xg, t * 16 + 16)
                dve.scalar_tensor_tensor(out=x_tile, in0=second, scalar=0.0, in1=x_tile, op0=ALU.max, op1=ALU.add).then_inc(s_x1, 1)
                yield 1
                dve.wait_ge(s_x1, t + 1)
                moments_of(x_tile)
                yield 2
                normalise(normed, x_tile, 2).then_inc(s_y, 1)
                yield 1
                dve.wait_ge(s_y, t + 1)
                moments_of(normed)
                yield 2
                normalise(agg[:, cols], normed, 3)
                yield 2
                dve.wait_ge(s_lg, t + 1)
                dve.tensor_tensor(logits[:, bass.ds(t * E, E)], bank[5][:, 0:E], br_row, ALU.add).then_inc(s_lt, 1)
                assert own.n == PER_TILE, own.n

            def tiles_of(i):
                return nc.values_load_multi_w_load_instructions(
                    lo_sb[0:1, bass.ds(i * RING, RING)], engines=[DVE], min_val=0, max_val=NT - 1,
                    skip_runtime_bounds_check_because="node numbers are below the padded count")[1]

            dve.wait_ge(s_param, 160)
            with dve.Fori(0, BORDER_PASSES) as i:
                tiles = tiles_of(i)
                for k in range(RING):
                    sum_step(i, k, tiles[k])
            tiles_done = dve.alloc_register("tiles_done_dve")
            dve.reg_mov(tiles_done, 0)
            with dve.Fori(0, SPANS) as i:
                tiles = first_tiles = tiles_of(i * 2 + BORDER_PASSES)
                with dve.If_lt(tiles_done, tiles[0]):
                    part = node_tile(dve.snap(tiles_done, min_val=0, max_val=NT - 1))
                    to_take = next(part)
                    for k in range(SPAN):
                        if k == RING:
                            tiles = tiles_of(i * 2 + (BORDER_PASSES + 1))
                        sum_step(i * 2 + (BORDER_PASSES + k // RING), k % RING, tiles[k % RING])
                        to_take -= 1
                        while to_take == 0:
                            to_take = next(part, None)
                            if to_take is None:
                                to_take = SPAN
                    for _ in part:
                        pass
                    dve.reg_add(tiles_done, tiles_done, 1)
                with dve.Else():
                    tiles = first_tiles
                    for k in range(SPAN):
                        if k == RING:
                            tiles = tiles_of(i * 2 + (BORDER_PASSES + 1))
                        sum_step(i * 2 + (BORDER_PASSES + k // RING), k % RING, tiles[k % RING])
            with dve.Fori(PASSES - REST_PASSES, PASSES) as i:
                tiles = tiles_of(i)
                for k in range(RING):
                    sum_step(i, k, tiles[k])
            dve.wait_ge(s_added, SUMS + STEPS)
            with dve.Fori(0, NT):
                with dve.If_lt(tiles_done, NT):
                    for _ in node_tile(dve.snap(tiles_done, min_val=0, max_val=NT - 1)):
                        pass
                    dve.reg_add(tiles_done, tiles_done, 1)
            dve.wait_ge(s_lt, NT)

            def te(view):
                return view.rearrange("p (t e) -> p t e", e=E)

            def over_experts(per_tok):
                return per_tok.rearrange("p (t e) -> p t e", e=1).to_broadcast([P, NT, E])

            def over_tokens(per_e):
                return per_e.rearrange("p (t e) -> p t e", t=1).to_broadcast([P, NT, E])

            top, total, key_top, denom = per_token
            chain(dve.tensor_reduce(top, te(logits[:, :]), AX_X, ALU.max))
            dve.tensor_tensor(te(work), te(logits[:, :]), over_experts(top), ALU.subtract).then_inc(s_shift, 1)
            rank = ahead[4]
            chain(dve.tensor_scalar(rank, iota[:, 0:E], -1.0, float(E), ALU.mult, ALU.add))
            dve.wait_ge(s_exp, 1)
            chain(dve.tensor_reduce(total, te(scores), AX_X, ALU.add))
            chain(dve.reciprocal(total, total))
            chain(dve.tensor_tensor(te(scores), te(scores), over_experts(total), ALU.mult))
            for c, onehot in enumerate((onehot0, onehot1)):
                weight = share[:, c * NT:(c + 1) * NT]
                chain(dve.tensor_reduce(weight, te(scores), AX_X, ALU.max))
                chain(dve.tensor_tensor(te(work), te(scores), over_experts(weight), ALU.is_equal))
                chain(dve.tensor_tensor(te(work), te(work), over_tokens(rank), ALU.mult))
                chain(dve.tensor_reduce(key_top, te(work), AX_X, ALU.max))
                chain(dve.tensor_tensor(te(onehot), te(work), over_experts(key_top), ALU.is_equal))
                if c == 0:
                    chain(dve.scalar_tensor_tensor(out=scores, in0=onehot, scalar=-2.0, in1=scores, op0=ALU.mult, op1=ALU.add))
            dve.tensor_tensor(both, onehot0, onehot1, ALU.add).then_inc(s_both, 1)
            chain(dve.tensor_tensor(denom, share[:, 0:NT], share[:, NT:2 * NT], ALU.add))
            chain(dve.reciprocal(denom, denom))
            for c in range(ROUTED):
                dve.tensor_tensor(share[:, c * NT:(c + 1) * NT], share[:, c * NT:(c + 1) * NT], denom, ALU.mult)
            dve.wait_ge(s_count, 2)
            chain(dve.tensor_copy(running, bank[1][:, 0:GE]))
            src_buf, dst_buf = running, other
            step = 1
            while step < NT:
                dve.tensor_copy(dst_buf[:, 0:step * E], src_buf[:, 0:step * E])
                chain(dve.tensor_tensor(dst_buf[:, step * E:GE], src_buf[:, step * E:GE], src_buf[:, 0:GE - step * E], ALU.add))
                src_buf, dst_buf = dst_buf, src_buf
                step *= 2
            tiles_f, tiles_i, end, end2 = ahead[:4]
            chain(dve.tensor_scalar(tiles_i.bitcast(I32), src_buf[:, GE - E:GE], float(P - 1), None, ALU.add))
            chain(dve.tensor_scalar(tiles_i.bitcast(I32), tiles_i.bitcast(I32), 7, None, ALU.arith_shift_right))
            chain(dve.tensor_copy(tiles_f, tiles_i.bitcast(I32)))
            a, b = tiles_f, end
            step = 1
            spare = [end, end2, tiles_i]
            for dst in spare:
                dve.tensor_copy(dst[:, 0:step], a[:, 0:step])
                chain(dve.tensor_tensor(dst[:, step:E], a[:, step:E], a[:, 0:E - step], ALU.add))
                a, step = dst, step * 2
            ends_e = a
            start_e = end
            chain(dve.tensor_tensor(start_e, ends_e, tiles_f, ALU.subtract))
            chain(dve.tensor_scalar(start_e, start_e, float(P), None, ALU.mult))
            chain(dve.tensor_tensor(dst_buf, src_buf, bank[1][:, 0:GE], ALU.subtract))
            chain(dve.tensor_tensor(dst_buf, dst_buf, bank[0][:, 0:GE], ALU.add))
            chain(dve.tensor_tensor(te(dst_buf), te(dst_buf), over_tokens(start_e), ALU.add))
            for c, onehot in enumerate((onehot0, onehot1)):
                chain(dve.tensor_tensor(work, onehot, dst_buf, ALU.mult))
                chain(dve.tensor_reduce(total, te(work), AX_X, ALU.add))
                chain(dve.tensor_copy(place[:, c * NT:(c + 1) * NT], total))
            j_of = iota.rearrange("p (j e) -> p j e", e=1).to_broadcast([P, P, E])
            chain(dve.tensor_tensor(ends.rearrange("p (j e) -> p j e", e=E), j_of,
                                    ends_e.rearrange("p (j e) -> p j e", j=1).to_broadcast([P, P, E]), ALU.is_ge))
            chain(dve.tensor_reduce(expert_f, ends.rearrange("p (j e) -> p j e", e=E), AX_X, ALU.add))
            dve.tensor_scalar(tile_expert[:, :], expert_f, float(E - 1), None, ALU.min).then_inc(s_routed, 1)
            dve.wait_ge(s_routed, 1)

            def stage_rows(g, first):
                for k in range(GROUP):
                    if not first:
                        dve.wait_ge(s_sent[k], g * (16 * ROUTED))
                    dve.tensor_copy(place_stage.rearrange("p (c k) -> p c k", c=ROUTED)[:, :, k:k + 1],
                                    place[:, :].rearrange("p (c t) -> p c t", c=ROUTED)[:, :, bass.ds(g * GROUP + k, 1)])
                    dve.tensor_copy(row_stage[:, k, :], agg[:, bass.ds((g * GROUP + k) * D, D)]).then_inc(s_row, 1)

            stage_rows(0, True)
            with dve.Fori(1, NG) as g:
                stage_rows(g, False)

            dve.wait_ge(s_weights, 32 * E)

            def scale_rows(j, r, e):
                dve.wait_ge(s_xt, j + 1)
                for c in range(DC):
                    at = bass.ds(e * DC + c, 1)
                    ins = dve.tensor_scalar(xt[:, r, c * P:(c + 1) * P], bank[4][:, c * P:(c + 1) * P], ln_g_col[:, at], ln_b_col[:, at], ALU.mult, ALU.add)
                ins.then_inc(s_xs, 1)

            def add_bias(j, r, m):
                dve.wait_ge(s_bias[r], m * 16 + 16)
                for half in range(2):
                    cols = slice(half * BOUND, (half + 1) * BOUND)
                    dve.wait_ge(s_f1, j * 2 + half + 1)
                    dve.tensor_tensor(hid[:, cols], bank[2 + half][:, :], bias[:, r, cols], ALU.add).then_inc(s_hb, 1)

            def take_output(j, r):
                dve.wait_ge(s_y_free, j + 1)
                dve.wait_ge(s_f2, j + 1)
                dve.tensor_tensor(y_sb[:, r, :], bank[5][:, 0:D], bias[:, r, FF:FF + D], ALU.add).then_inc(s_ys, 1)

            dve.sem_inc(s_y_free, 2)
            dve.sem_inc(s_ys, 1)
            e0, e1 = (dve.value_load(tile_expert[0:1, n:n + 1], min_val=0, max_val=E - 1) for n in range(2))
            scale_rows(0, 0, e0)
            add_bias(0, 0, 0)
            scale_rows(1, 1, e1)

            def slot_tile(j, r, m, m_next, e_after):
                if m_next is not None:
                    add_bias(j + 1, 1 - r, m_next)
                if e_after is not None:
                    scale_rows(j + 2, r, e_after)
                take_output(j, r)

            with dve.Fori(0, PAIRS) as i:
                _, e = nc.values_load_multi_w_load_instructions(tile_expert[0:1, bass.ds(i * 2, 4)], engines=[DVE], min_val=0, max_val=E - 1)
                slot_tile(i * 2, 0, i, i, e[2])
                slot_tile(i * 2 + 1, 1, i, i + 1, e[3])
            for j in range(2 * PAIRS, SLOT_TILES):
                e_after = dve.value_load(tile_expert[0:1, j + 2:j + 3], min_val=0, max_val=E - 1) if j + 2 < SLOT_TILES else None
                slot_tile(j, j % 2, j // 2, (j + 1) // 2 if j + 1 < SLOT_TILES else None, e_after)

            with dve.Fori(0, NG) as g:
                dve.wait_ge(s_x1g, g * 16 + 16)
                for k in range(GROUP):
                    dve.wait_ge(s_pair[k], g * (16 * ROUTED) + 16 * ROUTED)
                    cols = slice(k * D, (k + 1) * D)
                    for c, y in enumerate((first_y, second_y)):
                        ins = dve.scalar_tensor_tensor(out=x1_group[:, cols], in0=y[:, k, :], scalar=share[:, bass.ds(g * GROUP + (c * NT + k), 1)],
                                                       in1=x1_group[:, cols], op0=ALU.mult, op1=ALU.add)
                        if c == 0:
                            ins.then_inc(s_half, 1)
                            dve.wait_ge(s_half, g * GROUP + k + 1)
                    ins.then_inc(s_sum, 1)


def kernel(**inputs):
    import numpy as np
    import concourse.bacc as bacc
    from concourse.bass_utils import run_bass_kernel_spmd as run

    inp = {k: np.asarray(v) for k, v in inputs.items()}
    N, D = inp["x"].shape
    nodes = -(-N // P) * P
    x = np.zeros((nodes, D), np.float32)
    x[:N] = inp["x"]
    edges = inp["src"].shape[0]
    tiles = -(-edges // (P * RING)) * RING

    def rows(a, fill):
        b = np.full((tiles * P,), fill, a.dtype)
        b[:edges] = a
        return b.reshape(tiles, P)

    src, dst, wgt = rows(inp["src"], 0), rows(inp["dst"], nodes - 1), rows(inp["edge_weight"], 0)
    k = np.arange(P, dtype=np.float32)
    consts = np.concatenate([np.eye(P), k[:, None] < k[None, :], np.tile(k, (P, 1)), np.ones((P, P)), k[:, None] + 1], axis=1).astype(np.float32)

    def tcol(a, w):
        return np.ascontiguousarray(a.reshape(-1, P).T)

    arrays = {
        "x": x, "src_rows": src, "dst_rows": dst, "weight_rows": wgt,
        "src_cols": np.ascontiguousarray(src.T), "dst_cols": np.ascontiguousarray(dst.T), "weight_cols": np.ascontiguousarray(wgt.T),
        "epsilon": inp["L0_gnn_epsilon"],
        "w1t": np.ascontiguousarray(inp["L0_gnn_w1"].T), "w2t": np.ascontiguousarray(inp["L0_gnn_w2"].T),
        "gnn_rows": np.concatenate([inp["L0_gnn_b1"], inp["L0_gnn_b2"], inp["L0_gnn_g2"], inp["L0_gnn_beta2"]])[None],
        "g1t": tcol(inp["L0_gnn_g1"], 4), "beta1t": tcol(inp["L0_gnn_beta1"], 4),
        "wr": inp["L0_ffn_Wr"], "br": inp["L0_ffn_br"][None],
        "ln_gt": tcol(inp["L0_ffn_ln_g"], 16), "ln_bt": tcol(inp["L0_ffn_ln_b"], 16),
        "expert_w1": inp["L0_ffn_W1"], "expert_w2": inp["L0_ffn_W2"],
        "expert_bias": np.concatenate([inp["L0_ffn_b1"], inp["L0_ffn_b2"]], axis=1),
        "consts": consts,
    }
    arrays = {n: np.ascontiguousarray(a) for n, a in arrays.items()}
    nc = bacc.Bacc("TRN2", target_bir_lowering=False, num_devices=1)
    args = [nc.dram_tensor(n, a.shape, mybir.dt.from_np(a.dtype), kind="ExternalInput").ap() for n, a in arrays.items()]
    out = nc.dram_tensor("out", (nodes, D), F32, kind="ExternalOutput").ap()
    gnn_moe(nc, *args, out)
    r = run(nc, [arrays], core_ids=[0])
    return r.results[0]["out"][:N]
```

```python
from contextlib import ExitStack

import concourse.bass as bass
from concourse import mybir

P = 128
F32 = mybir.dt.float32
I32 = mybir.dt.int32
ALU = mybir.AluOpType
ACT = mybir.ActivationFunctionType
AX_X = mybir.AxisListType.X
DVE = mybir.EngineType.DVE
LN_EPS = 1e-5
RING = 16
FREED = 4
SPAN = 2 * RING
SELS = 8
SUMS = 4
GROUP = 7
ROUTED = 2
HOTS = 4


class Chain:

    def __init__(self, eng, sem):
        self.eng, self.sem, self.n, self.before = eng, sem, 0, 0

    def __call__(self, ins):
        self.n += 1
        ins.then_inc(self.sem, 1)
        self.eng.wait_ge(self.sem, self.before + self.n)

    def enter(self, i, per):
        self.before = i * per


def interleave(node_work, sum_step, steps, share):
    ahead = next(node_work)
    for n in range(steps):
        sum_step(n)
        ahead -= share
        while ahead <= 0:
            ahead += next(node_work, 2 * SPAN)
    for _ in node_work:
        pass


def gnn_moe(nc, x, src_rows, dst_rows, weight_rows, src_cols, dst_cols, next_dst_cols, weight_cols, epsilon,
            w1t, w2t, gnn_rows, g1t, beta1t, wr, br, ln_gt, ln_bt, expert_w1, expert_w2,
            expert_b1t, expert_b2, consts, out):
    NODES, D = x.shape
    NT = NODES // P
    NG = NT // GROUP
    ET = src_rows.shape[0]
    STEPS = ET + NT - 1
    PASSES = STEPS // RING
    BORDER_PASSES = (NT - 1) // RING
    SPANS = ET // SPAN
    REST_PASSES = (ET - SPANS * SPAN) // RING
    TAIL_TILES = 2
    HID = w1t.shape[1]
    DC, HC = D // P, HID // P
    E, _, FF = expert_w1.shape
    FC = FF // P
    SLOT_TILES = (ROUTED * NODES + E * (P - 1)) // P
    BOUND = 512
    assert ET % RING == 0 and STEPS % (2 * SPAN) == 0 and (NT - 1) % RING == 0 and NG * GROUP == NT and D == 256 and FF == 1024

    x_scratch = nc.dram_tensor("normed_nodes", (NODES, D), F32, kind="Internal").ap()
    expert_in = nc.dram_tensor("expert_inputs", (NODES, D), F32, kind="Internal").ap()

    with ExitStack() as ctx:
        def sb(name, shape, dt=F32):
            return ctx.enter_context(nc.sbuf_tensor(name, shape, dt))

        def sem(name):
            return ctx.enter_context(nc.semaphore(name))

        region_a = sb("region_a", [P, E * DC * FF])
        region_b = sb("region_b", [P, E * FC * D])
        agg = sb("agg", [P, NT * D])
        const = sb("const", [P, 4 * P + 2])
        ident, before, iota, ones = (const[:, n * P:(n + 1) * P] for n in range(4))
        bank = [ctx.enter_context(nc.psum_tensor(f"bank{n}", [P, BOUND], F32)) for n in range(8)]

        xn = region_a[:, 0:NT * D]

        used = [0]

        def carve(n, dt=F32):
            at = used[0]
            used[0] += n
            assert used[0] <= E * FC * D
            view = region_b[:, at:at + n]
            return view if dt is F32 else view.bitcast(dt)

        w1_sb = sb("w1_sb", [P, DC * HID])
        w2_sb = sb("w2_sb", [P, HC * D])
        rows_sb = sb("rows_sb", [P, HID + 3 * D])
        b1_row, b2_row, g2_row, beta2_row = (rows_sb[:, a:b] for a, b in (
            (0, HID), (HID, HID + D), (HID + D, HID + 2 * D), (HID + 2 * D, HID + 3 * D)))
        small = sb("small", [P, 2 * HC + DC * E + E + 2 * E * DC + 1 + E * FC])
        at = 0
        views = []
        for width in (HC, HC, DC * E, E, E * DC, E * DC, 1, E * FC):
            views.append(small[:, at:at + width])
            at += width
        g1_col, beta1_col, wr_sb, br_row, ln_g_col, ln_b_col, eps_col, up_bias_col = views
        logits = sb("logits", [P, NT * E])
        share = sb("share", [P, ROUTED * NT])
        slot_from, slot_to = sb("slot_from", [P, SLOT_TILES], I32), sb("slot_to", [P, SLOT_TILES], I32)
        slot_share = sb("slot_share", [P, SLOT_TILES])
        tiles_used = sb("tiles_used", [P, 1], I32)
        tile_expert = sb("tile_expert", [P, P], I32)
        zeros = sb("zeros", [P, D])
        ln_eps = sb("ln_eps", [P, 1])
        in_order = sb("in_order", [P, 1], I32)

        COLS = STEPS + SPAN
        src_sb, lo_sb = carve(COLS, I32), carve(COLS, I32)
        rel_sb, wgt_sb, dstf = carve(COLS), carve(COLS), carve(ET)
        dst_sb = carve(ET, I32)
        gathered = carve(RING * D).rearrange("p (r d) -> p r d", r=RING)
        select = carve(SELS * P).rearrange("p (r d) -> p r d", r=SELS)
        staged = carve(2 * SPAN, I32)
        border = carve(3 * P + 3)
        border_rows = carve(3 * P)
        border_at = carve(1, I32)
        stats = carve(GROUP * 6)
        moments = carve(GROUP * 2)
        rstd, shift = carve(NT), carve(NT)
        fall_count, rel_now = carve(1), carve(1)

        at = NT * D
        views = []
        for width in (HID, HID, D, D, D, D, D, D, 6, 2, 1):
            views.append(region_a[:, at:at + width])
            at += width
        hidden, act1t, h0, h0t, second, x_tile, normed, yt, n_stats, n_moments, n_rstd = views
        assert at <= E * DC * FF
        next_dst = region_a[:, NT * D:NT * D + ET].bitcast(I32)
        falls = region_a[:, NT * D + ET:NT * D + 2 * ET]
        used[0] = 0
        scores, onehot0, onehot1, both, work, running, other = (carve(NT * E) for _ in range(7))
        per_token = [carve(NT) for _ in range(4)]
        ahead = [carve(E) for _ in range(5)]
        ends = carve(P * E)
        expert_f = carve(P)
        used_agg = [0]

        def carve_agg(n, dt=F32):
            at = used_agg[0]
            used_agg[0] += n
            assert used_agg[0] <= NT * D
            view = agg[:, at:at + n]
            return view if dt is F32 else view.bitcast(dt)

        x_in = carve_agg(2 * D).rearrange("p (r d) -> p r d", r=2)
        xt = carve_agg(2 * D).rearrange("p (r d) -> p r d", r=2)
        bias = carve_agg(2 * D).rearrange("p (r d) -> p r d", r=2)
        w1_now = carve_agg(2 * DC * FF).rearrange("p (r d) -> p r d", r=2)
        hid_t = carve_agg(2 * FF).rearrange("p (r d) -> p r d", r=2)
        y_sb = carve_agg(2 * D).rearrange("p (r d) -> p r d", r=2)
        from_now, to_now = carve_agg(2, I32), carve_agg(2, I32)
        slot, slot_int = carve_agg(ROUTED * NT), carve_agg(ROUTED * NT, I32)
        row_and_col = carve_agg(NT * ROUTED * 2)
        token_next = carve_agg(NT)
        col_values = carve_agg(HOTS * ROUTED * 2 * SLOT_TILES).rearrange("p (b c n) -> p b c n", b=HOTS, c=ROUTED)
        hot = w1_now.rearrange("p r d -> p (r d)")[:, 0:HOTS * ROUTED * 2 * P].rearrange("p (b c k n) -> p b c k n", b=HOTS, c=ROUTED, k=2)
        empty, past_nodes = carve_agg(SLOT_TILES), carve_agg(SLOT_TILES)
        w1_all = region_a
        w2_all = region_b

        s_const = sem("const_loaded")
        s_edges = sem("edges_loaded")
        s_x = [sem(f"x_loaded{g}") for g in range(NG)]
        s_dst = sem("destinations_loaded")
        s_agg_clear = sem("sums_cleared")
        s_falls, s_fall_count, s_order = sem("falls_counted"), sem("fall_count_ready"), sem("order_known")
        s_any_free, s_any_staged, s_any_gathered, s_any_select, s_any_partial, s_any_own = (sem(f"unsorted_{n}") for n in (
            "edges_done", "index_staged", "gathered", "selection_ready", "partial_sum_ready", "step"))
        s_dve = sem("dve_step")
        s_sqrt_in = sem("variance_ready")
        s_sqrt = sem("deviation_ready")
        s_scaling = sem("scale_and_shift_ready")
        s_xn = sem("normed_ready")
        s_xn_stored = sem("normed_stored")
        s_dstf = sem("dst_float_ready")
        s_bcast = sem("first_dst_spread")
        s_border_at = sem("border_tile_known")
        s_border_rows = sem("border_rows_gathered")
        s_border_in = sem("border_rows_ready")
        s_border_t = sem("border_rows_turned")
        s_plan = sem("plan_ready")
        s_staged = sem("indices_staged")
        s_gather = [sem(f"gathered{n}") for n in range(RING)]
        s_select = sem("selection_ready")
        s_partial = sem("partial_sum_ready")
        s_added = sem("partial_sum_added")
        s_param = sem("parameters_loaded")
        s_zero = sem("zeros_ready")
        s_eps = sem("ln_eps_ready")
        s_pad = sem("rows_past_nodes_cleared")
        s_rows_stored = sem("expert_inputs_stored")
        s_xg = sem("x_tile_loaded")
        s_x1 = sem("x1_ready")
        s_node = sem("node_layer_step")
        s_x1_stored = sem("x1_stored")
        s_h0, s_h0t, s_h0c, s_m1 = (sem(n) for n in ("h0_ready", "h0_turned", "h0_copied", "product1_ready"))
        s_var, s_dev = sem("row_variance_ready"), sem("row_deviation_ready")
        s_z1, s_z1t, s_a1, s_m2 = (sem(n) for n in ("z1_ready", "z1_turned", "act1_ready", "product2_ready"))
        s_y, s_yt, s_yc, s_lg, s_lt = (sem(n) for n in ("y_ready", "y_turned", "y_copied", "logits_ready", "logits_taken"))
        s_shift, s_exp, s_both, s_count, s_routed = (sem(n) for n in ("shifted_ready", "exponentials_ready", "choice_ready", "counts_ready", "routing_ready"))
        s_hot, s_token, s_share, s_used, s_slots = (sem(n) for n in (
            "slot_onehots_ready", "token_columns_ready", "share_columns_ready", "slot_onehots_used", "slot_lists_ready"))
        s_spare = sem("nobody_waits")
        s_weights = sem("expert_weights_loaded")
        s_xin = [sem(f"slot_rows_loaded{r}") for r in range(2)]
        s_bias = [sem(f"bias_loaded{r}") for r in range(2)]
        s_xt, s_xs, s_w1_now, s_f1, s_ge, s_f2, s_ys = (sem(n) for n in (
            "slot_rows_turned", "slot_rows_scaled", "up_weights_in_place", "up_ready", "gelu_ready", "down_ready", "down_biased"))
        s_y_free = sem("slot_output_added_and_free")
        s_y_added = [sem(f"slot_output_added{r}") for r in range(2)]
        s_from, s_to = sem("gather_index_staged"), sem("scatter_index_staged")
        s_yw = sem("slot_output_weighted")

        block = ctx.enter_context(nc.Block())

        def group_rows(dram, g):
            return dram[bass.ds(g * (GROUP * P), GROUP * P), :].rearrange("(t p) d -> p t d", p=P)

        def tiled(view):
            return view.rearrange("p (t d) -> p t d", d=D)

        PER_TILE = 13
        SHARED = 4
        PARAMS = 11
        LOOKED = 2
        AHEAD = 2 * LOOKED
        PAIRS = (SLOT_TILES - LOOKED) // 2

        def last_tiles(eng, name):
            in_loop = eng.alloc_register(f"in_loop_{name}")
            eng.reg_mov(in_loop, 2 * PAIRS)
            return eng.If_lt(in_loop, eng.value_load(tiles_used[0:1, 0:1], min_val=0, max_val=SLOT_TILES))

        def over_tiles(eng, body):
            assert NT % HOTS == 1
            for t in range(HOTS):
                body(t, t)
            with eng.Fori(1, (NT - 1) // HOTS) as i:
                for b in range(HOTS):
                    body(i * HOTS + b, b)
            body(NT - 1, 0)

        @block.sync
        def _(sp):
            def load_x(g):
                sp.dma_start(tiled(xn[:, g * GROUP * D:(g + 1) * GROUP * D]), group_rows(x, g)).then_inc(s_x[g], 16)

            load_x(0)
            sp.dma_start(dst_sb, dst_cols).then_inc(s_dst, 16)
            sp.dma_start(next_dst, next_dst_cols).then_inc(s_dst, 16)
            sp.dma_start(const[:, :], consts).then_inc(s_const, 16)
            load_x(1)
            for dst, src in ((src_sb, src_cols), (wgt_sb, weight_cols)):
                sp.dma_start(dst[:, NT - 1:STEPS], src).then_inc(s_edges, 16)
            for g in range(2, NG):
                load_x(g)
            for g in range(NG):
                sp.wait_ge(s_xn, g + 1 if g < NG - 1 else NG + 1)
                sp.dma_start(group_rows(x_scratch, g), tiled(xn[:, g * GROUP * D:(g + 1) * GROUP * D])).then_inc(s_xn_stored, 16)
            params = ((w1_sb[:, :].rearrange("p (c n) -> p c n", c=DC), w1t.rearrange("(c p) n -> p c n", p=P)),
                      (w2_sb[:, :].rearrange("p (c n) -> p c n", c=HC), w2t.rearrange("(c p) n -> p c n", p=P)),
                      (rows_sb[:, :], gnn_rows.to_broadcast([P, HID + 3 * D])), (g1_col, g1t), (beta1_col, beta1t),
                      (wr_sb.rearrange("p (c n) -> p c n", c=DC), wr.rearrange("(c p) n -> p c n", p=P)),
                      (br_row, br.to_broadcast([P, E])), (ln_g_col, ln_gt), (ln_b_col, ln_bt),
                      (eps_col, epsilon.to_broadcast([P, 1])), (up_bias_col, expert_b1t))
            assert len(params) == PARAMS
            for dst, src in params:
                sp.dma_start(dst, src).then_inc(s_param, 16)
            sp.wait_ge(s_zero, 1)
            sp.dma_start(out[NODES:NODES + P, :], zeros[:, :]).then_inc(s_pad, 16)

            def node_rows(dram, t):
                return dram[bass.ds(t * P, P), :]

            sp.dma_start(x_tile, node_rows(x, 0)).then_inc(s_xg, 16)
            with sp.Fori(0, NT - 1) as t:
                sp.wait_ge(s_x1, t + 1)
                sp.dma_start(node_rows(out, t), x_tile).then_inc(s_x1_stored, 16)
                sp.wait_ge(s_x1_stored, t * 16 + 16)
                sp.wait_ge(s_y, t + 1)
                sp.dma_start(x_tile, node_rows(x, t + 1)).then_inc(s_xg, 16)
                sp.wait_ge(s_lt, t + 1)
                sp.dma_start(node_rows(expert_in, t), agg[:, bass.ds(t * D, D)]).then_inc(s_rows_stored, 16)
            sp.wait_ge(s_x1, NT)
            sp.dma_start(node_rows(out, NT - 1), x_tile).then_inc(s_x1_stored, 16)
            sp.wait_ge(s_lt, NT)
            sp.dma_start(node_rows(expert_in, NT - 1), agg[:, (NT - 1) * D:NT * D]).then_inc(s_rows_stored, 16)

            sp.wait_ge(s_x1_stored, 16 * NT)
            for e in range(E):
                sp.dma_start(w1_all[:, e * DC * FF:(e + 1) * DC * FF].rearrange("p (c n) -> p c n", c=DC),
                             expert_w1[e].rearrange("(c p) n -> p c n", p=P)).then_inc(s_weights, 16)
            sp.wait_ge(s_routed, 1)
            for e in range(E):
                sp.dma_start(w2_all[:, e * FC * D:(e + 1) * FC * D].rearrange("p (c n) -> p c n", c=FC),
                             expert_w2[e].rearrange("(c p) n -> p c n", p=P)).then_inc(s_weights, 16)

            def load_bias(j, r):
                e = sp.value_load(tile_expert[0:1, bass.ds(j, 1)], min_val=0, max_val=E - 1)
                sp.dma_start(bias[:, r, :], expert_b2[bass.ds(e, 1), :].to_broadcast([P, D])).then_inc(s_bias[r], 16)

            def slot_tile(j, r, m):
                more = not isinstance(j, int) or j + LOOKED < SLOT_TILES
                if more:
                    sp.wait_ge(s_ys, j + 2)
                    load_bias(j + LOOKED, r)
                    sp.wait_ge(s_y_added[r], m * 16 + 16)
                    sp.sem_inc(s_y_free, 1)

            sp.wait_ge(s_rows_stored, 16 * NT)
            for j in range(LOOKED):
                load_bias(j, j)
            with sp.Fori(0, PAIRS) as i:
                for r in range(2):
                    slot_tile(i * 2 + r, r, i)
            with last_tiles(sp, "sp"):
                for j in range(2 * PAIRS, SLOT_TILES):
                    slot_tile(j, j % 2, j // 2)
                for r in range(2):
                    sp.wait_ge(s_y_added[r], 16 * ((SLOT_TILES + 1 - r) // 2))
            for r in range(2):
                sp.wait_ge(s_bias[r], 16 * (PAIRS + 1))

        @block.scalar
        def _(act):
            act.wait_ge(s_eps, 1)
            for g in range(NG):
                of_group = slice(g * GROUP, (g + 1) * GROUP)
                act.wait_ge(s_sqrt_in, g + 1)
                nc.scalar.activation(rstd[:, of_group], moments[:, 1::2], ACT.Sqrt, bias=ln_eps[:, :]).then_inc(s_sqrt, 1)
                act.wait_ge(s_scaling, g + 1)
                for t in range(g * GROUP, (g + 1) * GROUP - (SHARED if g == NG - 1 else 0)):
                    rows = xn[:, t * D:(t + 1) * D]
                    ins = nc.scalar.activation(rows, rows, ACT.Identity, bias=shift[:, t:t + 1], scale=rstd[:, t:t + 1])
                ins.then_inc(s_xn, 1)
            act.wait_ge(s_param, 16 * PARAMS)

            def deviation(t, n):
                act.wait_ge(s_var, t * 4 + n + 1)
                nc.scalar.activation(n_rstd, n_moments[:, 1:2], ACT.Sqrt, bias=ln_eps[:, :]).then_inc(s_dev, 1)

            def node_tile(t):
                act.wait_ge(s_h0t, t + 1)
                nc.scalar.copy(h0t, bank[4][:, 0:D]).then_inc(s_h0c, 1)
                deviation(t, 0)
                act.wait_ge(s_z1t, t + 1)
                for c in range(HC):
                    ins = nc.scalar.activation(act1t[:, c * P:(c + 1) * P], bank[6][:, c * P:(c + 1) * P], ACT.Relu,
                                               bias=beta1_col[:, c:c + 1], scale=g1_col[:, c:c + 1])
                ins.then_inc(s_a1, 1)
                deviation(t, 1)
                deviation(t, 2)
                act.wait_ge(s_yt, t + 1)
                nc.scalar.copy(yt, bank[4][:, 0:D]).then_inc(s_yc, 1)
                deviation(t, 3)

            act.wait_ge(s_plan, 1)
            with act.Fori(0, NT) as t:
                node_tile(t)

            act.wait_ge(s_shift, 1)
            nc.scalar.activation(scores, work, ACT.Exp).then_inc(s_exp, 1)

            def token_columns(t, b):
                act.wait_ge(s_hot, t + 1)
                act.sem_inc(s_spare, 1)
                for c in range(ROUTED):
                    ins = nc.scalar.activation(col_values[:, b, c, 0:SLOT_TILES], hot[:, b, c, 1, 0:SLOT_TILES], ACT.Identity,
                                               scale=token_next[:, bass.ds(t, 1)])
                ins.then_inc(s_token, 1)

            over_tiles(act, token_columns)

            def slot_tile(j, r, e):
                for half in range(2):
                    act.wait_ge(s_f1, j * 2 + half + 1)
                    act.sem_inc(s_spare, 1)
                    for c in range(4):
                        at = half * 4 + c
                        ins = nc.scalar.activation(hid_t[:, r, at * P:(at + 1) * P], bank[2 * r + half][:, c * P:(c + 1) * P], ACT.Gelu,
                                                   bias=up_bias_col[:, bass.ds(e * FC + at, 1)])
                    ins.then_inc(s_ge, 1)

            act.wait_ge(s_routed, 1)
            with act.Fori(0, PAIRS) as i:
                for r in range(2):
                    e = act.value_load(tile_expert[0:1, bass.ds(i * 2 + r, 1)], min_val=0, max_val=E - 1)
                    slot_tile(i * 2 + r, r, e)
            with last_tiles(act, "act"):
                for j in range(2 * PAIRS, SLOT_TILES):
                    slot_tile(j, j % 2, act.value_load(tile_expert[0:1, j:j + 1], min_val=0, max_val=E - 1))

        @block.gpsimd
        def _(pool):
            nc.gpsimd.memset(zeros[:, :], 0.0).then_inc(s_zero, 1)
            nc.gpsimd.memset(ln_eps[:, :], LN_EPS).then_inc(s_eps, 1)
            nc.gpsimd.memset(agg[:, :], 0.0).then_inc(s_agg_clear, 1)
            pool.wait_ge(s_border_at, 1)
            for n, rows in enumerate((src_rows, dst_rows, weight_rows)):
                dst = border_rows[:, n * P:(n + 1) * P]
                pool.indirect_dma_start(dst[0:NT - 1, :] if n == 2 else dst[0:NT - 1, :].bitcast(I32), None, rows,
                                        bass.IndirectOffsetOnAxis(ap=border_at[0:NT - 1, :], axis=0)).then_inc(s_border_rows, 16)
            pool.wait_ge(s_xn_stored, 16 * NG)
            pool.wait_ge(s_plan, 1)
            pool.wait_ge(s_order, 1)
            nothing = pool.alloc_register("nothing")
            pool.reg_mov(nothing, 0)
            order = pool.value_load(in_order[0:1, 0:1], min_val=0, max_val=1)
            with pool.If_lt(nothing, order):
                def stage(first, half):
                    nc.gpsimd.tensor_copy(staged[:, half * SPAN:(half + 1) * SPAN], src_sb[:, bass.ds(first, SPAN)]).then_inc(s_staged, 1)

                stage(0, 0)
                with pool.Fori(0, STEPS // (2 * SPAN)) as i:
                    for half in range(2):
                        now = staged[:, half * SPAN:(half + 1) * SPAN]
                        pool.wait_ge(s_staged, i * 2 + half + 1)
                        for n in range(SPAN):
                            if n == RING + FREED:
                                stage(i * (2 * SPAN) + (half + 1) * SPAN, 1 - half)
                            if n % FREED == 0:
                                pool.wait_ge(s_partial, i * (2 * SPAN) + (half * SPAN + n + FREED))
                                pool.sem_inc(s_spare, 1)
                            pool.indirect_dma_start(gathered[:, n % RING, :], None, x_scratch,
                                                    bass.IndirectOffsetOnAxis(ap=now[:, n:n + 1], axis=0)).then_inc(s_gather[n % RING], 16)
            with pool.Else():
                with pool.Fori(0, ET) as t:
                    pool.wait_ge(s_any_free, t + 1)
                    nc.gpsimd.tensor_copy(staged[:, 0:1], src_sb[:, bass.ds(t + (NT - 1), 1)]).then_inc(s_any_staged, 1)
                    pool.wait_ge(s_any_staged, t + 1)
                    pool.sem_inc(s_spare, 1)
                    pool.indirect_dma_start(gathered[:, 0, :], None, x_scratch,
                                            bass.IndirectOffsetOnAxis(ap=staged[:, 0:1], axis=0)).then_inc(s_any_gathered, 16)

            def share_columns(t, b):
                pool.wait_ge(s_hot, t + 1)
                pool.sem_inc(s_spare, 1)
                nc.gpsimd.tensor_tensor(col_values[:, b, :, SLOT_TILES:2 * SLOT_TILES], hot[:, b, :, 1, 0:SLOT_TILES],
                                        share[:, :].rearrange("p (c t) -> p c t", c=ROUTED)[:, :, bass.ds(t, 1)].to_broadcast([P, ROUTED, SLOT_TILES]),
                                        ALU.mult).then_inc(s_share, 1)

            over_tiles(pool, share_columns)

            def gather_rows(j, r):
                nc.gpsimd.tensor_copy(from_now[:, r:r + 1], slot_from[:, bass.ds(j, 1)]).then_inc(s_from, 1)
                pool.wait_ge(s_from, j + 1)
                pool.sem_inc(s_spare, 1)
                pool.indirect_dma_start(x_in[:, r, :], None, expert_in, bass.IndirectOffsetOnAxis(ap=from_now[:, r:r + 1], axis=0)).then_inc(s_xin[r], 16)

            def add_outputs(j, r, m_last):
                if m_last is not None:
                    pool.wait_ge(s_y_added[1 - r], m_last * 16 + 16)
                    pool.sem_inc(s_spare, 1)
                nc.gpsimd.tensor_copy(to_now[:, r:r + 1], slot_to[:, bass.ds(j, 1)]).then_inc(s_to, 1)
                pool.wait_ge(s_to, j + 1)
                pool.wait_ge(s_yw, j + 1)
                pool.sem_inc(s_spare, 1)
                pool.indirect_dma_start(out, bass.IndirectOffsetOnAxis(ap=to_now[:, r:r + 1], axis=0), y_sb[:, r, :], None,
                                        compute_op=ALU.add).then_inc(s_y_added[r], 16)

            def slot_tile(j, r, m_last):
                if not isinstance(j, int) or j + AHEAD < SLOT_TILES:
                    pool.wait_ge(s_xt, j + (LOOKED + 1))
                    pool.sem_inc(s_spare, 1)
                    gather_rows(j + AHEAD, r)
                add_outputs(j, r, m_last)

            pool.wait_ge(s_rows_stored, 16 * NT)
            pool.wait_ge(s_x1_stored, 16 * NT)
            pool.wait_ge(s_pad, 16)
            pool.wait_ge(s_slots, 2)
            for j in range(AHEAD):
                if j >= LOOKED:
                    pool.wait_ge(s_xt, j - LOOKED + 1)
                gather_rows(j, j % 2)
            slot_tile(0, 0, None)
            POOL_PAIRS = (SLOT_TILES - AHEAD - 1) // 2
            with pool.Fori(0, POOL_PAIRS) as i:
                slot_tile(i * 2 + 1, 1, i)
                slot_tile(i * 2 + 2, 0, i)
            for j in range(2 * POOL_PAIRS + 1, 2 * PAIRS):
                slot_tile(j, j % 2, (j - 1) // 2)
            with last_tiles(pool, "pool"):
                for j in range(2 * PAIRS, SLOT_TILES):
                    slot_tile(j, j % 2, (j - 1) // 2)
            for r in range(2):
                pool.wait_ge(s_xin[r], 16 * ((SLOT_TILES + 1 - r) // 2))

        @block.tensor
        def _(pe):
            pe.sem_inc(s_partial, RING)
            pe.wait_ge(s_const, 16)
            pe.wait_ge(s_dstf, 1)
            CH = ET // 4
            for n in range(4):
                nc.tensor.matmul(bank[n][:, 0:CH], ones[0:1, :], dstf[0:1, n * CH:(n + 1) * CH], start=True, stop=True).then_inc(s_bcast, 1)
            pe.wait_ge(s_falls, 1)
            nc.tensor.matmul(bank[7][:, 0:1], ones, fall_count, start=True, stop=True).then_inc(s_fall_count, 1)
            pe.wait_ge(s_border_in, 1)
            for n in range(3):
                nc.tensor.transpose(bank[4 + n][:, 0:NT - 1], border[0:NT - 1, n * P:(n + 1) * P], ident[0:NT - 1, 0:NT - 1]).then_inc(s_border_t, 1)

            def turn(dst, src, chunks):
                for c in range(chunks):
                    ins = nc.tensor.transpose(dst[:, c * P:(c + 1) * P], src[:, c * P:(c + 1) * P], ident)
                return ins

            def sum_step(i, k):
                pe.wait_ge(s_select, i * RING + k + 1)
                pe.wait_ge(s_gather[k], i * 16 + 16)
                pe.wait_ge(s_added, i * RING + k + 1)
                nc.tensor.matmul(bank[k % SUMS][:, 0:D], select[:, k % SELS, :], gathered[:, k, :], start=True, stop=True).then_inc(s_partial, 1)

            def node_tile(t):
                yield 4
                pe.wait_ge(s_h0, t + 1)
                turn(bank[4], h0, DC).then_inc(s_h0t, 1)
                for c in range(DC):
                    yield 2 - c
                    if c == 0:
                        pe.wait_ge(s_h0c, t + 1)
                    ins = nc.tensor.matmul(bank[5][:, 0:HID], h0t[:, c * P:(c + 1) * P], w1_sb[:, c * HID:(c + 1) * HID], start=(c == 0), stop=(c == DC - 1))
                ins.then_inc(s_m1, 1)
                yield 5
                pe.wait_ge(s_z1, t + 1)
                turn(bank[6], hidden, HC).then_inc(s_z1t, 1)
                yield 2
                for c in range(HC):
                    yield 1
                    if c == 0:
                        pe.wait_ge(s_a1, t + 1)
                    ins = nc.tensor.matmul(bank[7][:, 0:D], act1t[:, c * P:(c + 1) * P], w2_sb[:, c * D:(c + 1) * D], start=(c == 0), stop=(c == HC - 1))
                ins.then_inc(s_m2, 1)
                yield 9
                pe.wait_ge(s_y, t + 1)
                turn(bank[4], normed, DC).then_inc(s_yt, 1)
                yield 2
                pe.wait_ge(s_yc, t + 1)
                for c in range(DC):
                    ins = nc.tensor.matmul(bank[5][:, 0:E], yt[:, c * P:(c + 1) * P], wr_sb[:, c * E:(c + 1) * E], start=(c == 0), stop=(c == DC - 1))
                ins.then_inc(s_lg, 1)

            tiles_done = pe.alloc_register("tiles_done_pe")
            pe.reg_mov(tiles_done, 0)
            pe.wait_ge(s_order, 1)
            order = pe.value_load(in_order[0:1, 0:1], min_val=0, max_val=1)
            with pe.If_lt(tiles_done, order):
                with pe.Fori(0, BORDER_PASSES) as i:
                    for k in range(RING):
                        sum_step(i, k)
                pe.wait_ge(s_param, 16 * PARAMS)
                def spread(passes, first_tile):
                    steps = len(passes) * RING

                    def step(n):
                        sum_step(passes[n // RING], n % RING)

                    with pe.If_lt(tiles_done, first_tile):
                        interleave(node_tile(pe.snap(tiles_done, min_val=0, max_val=NT - 1)), step, steps, SPAN // steps)
                        pe.reg_add(tiles_done, tiles_done, 1)
                    with pe.Else():
                        for n in range(steps):
                            step(n)

                with pe.Fori(0, SPANS) as i:
                    first_tile = pe.value_load(lo_sb[0:1, bass.ds(i * SPAN + (NT - 1), 1)], min_val=0, max_val=NT)
                    spread([i * 2 + BORDER_PASSES, i * 2 + (BORDER_PASSES + 1)], first_tile)
                for i in range(PASSES - REST_PASSES, PASSES):
                    first_tile = pe.value_load(lo_sb[0:1, i * RING:i * RING + 1], min_val=0, max_val=NT)
                    spread([i], first_tile)
            with pe.Else():
                pe.wait_ge(s_param, 16 * PARAMS)
                with pe.Fori(0, ET) as t:
                    pe.wait_ge(s_any_gathered, t * 16 + 16)
                    pe.sem_inc(s_spare, 1)
                    with pe.Fori(0, NT) as n:
                        pe.wait_ge(s_any_select, t * NT + n + 1)
                        nc.tensor.matmul(bank[0][:, 0:D], select[:, 0, :], gathered[:, 0, :], start=True, stop=True).then_inc(s_any_partial, 1)

            def rest_of_tiles(first, end):
                with pe.Fori(first, end):
                    with pe.If_lt(tiles_done, NT):
                        for _ in node_tile(pe.snap(tiles_done, min_val=0, max_val=NT - 1)):
                            pass
                        pe.reg_add(tiles_done, tiles_done, 1)

            rest_of_tiles(0, TAIL_TILES)
            with pe.If_lt(tiles_done, NT):
                rest_of_tiles(TAIL_TILES, NT)

            pe.wait_ge(s_both, 1)
            nc.tensor.matmul(bank[0][:, 0:NT * E], before, both, start=True, stop=True).then_inc(s_count, 1)
            nc.tensor.matmul(bank[1][:, 0:NT * E], ones, both, start=True, stop=True).then_inc(s_count, 1)

            def invert(t, b):
                pe.wait_ge(s_token, t + 1)
                pe.wait_ge(s_share, t + 1)
                for c in range(ROUTED):
                    start = isinstance(t, int) and t == 0 and c == 0
                    stop = isinstance(t, int) and t == NT - 1 and c == ROUTED - 1
                    ins = nc.tensor.matmul(bank[6][:, 0:2 * SLOT_TILES], hot[:, b, c, 0, :], col_values[:, b, c, :], start=start, stop=stop)
                ins.then_inc(s_used, 1)

            over_tiles(pe, invert)

            pe.wait_ge(s_weights, 16 * 2 * E)

            def turn_rows(j, r, m):
                pe.wait_ge(s_xin[r], m * 16 + 16)
                for c in range(DC):
                    ins = nc.tensor.transpose(bank[4][:, c * P:(c + 1) * P], x_in[:, r, c * P:(c + 1) * P], ident)
                ins.then_inc(s_xt, 1)

            def up(j, r):
                pe.wait_ge(s_xs, j + 1)
                pe.wait_ge(s_w1_now, j + 1)
                for half in range(2):
                    for n in range(4):
                        for c in range(DC):
                            at = c * FF + (half * 4 + n) * P
                            ins = nc.tensor.matmul(bank[2 * r + half][:, n * P:(n + 1) * P], w1_now[:, r, at:at + P], xt[:, r, c * P:(c + 1) * P],
                                                   start=(c == 0), stop=(c == DC - 1))
                    ins.then_inc(s_f1, 1)

            def down(j, r, e):
                pe.wait_ge(s_ys, j + 1)
                for c in range(FC):
                    if c % 4 == 0:
                        pe.wait_ge(s_ge, j * 2 + c // 4 + 1)
                    w = w2_all[:, bass.ds(e * (FC * D) + c * D, D)]
                    ins = nc.tensor.matmul(bank[5][:, 0:D], hid_t[:, r, c * P:(c + 1) * P], w, start=(c == 0), stop=(c == FC - 1))
                ins.then_inc(s_f2, 1)

            turn_rows(0, 0, 0)
            up(0, 0)
            turn_rows(1, 1, 0)

            def slot_tile(j, r, m, e):
                if not isinstance(j, int) or j + 1 < SLOT_TILES:
                    up(j + 1, 1 - r)
                if m is not None:
                    turn_rows(j + 2, r, m + 1)
                down(j, r, e)

            with pe.Fori(0, PAIRS) as i:
                for r in range(2):
                    e = pe.value_load(tile_expert[0:1, bass.ds(i * 2 + r, 1)], min_val=0, max_val=E - 1)
                    slot_tile(i * 2 + r, r, i, e)
            with last_tiles(pe, "pe"):
                for j in range(2 * PAIRS, SLOT_TILES):
                    e = pe.value_load(tile_expert[0:1, j:j + 1], min_val=0, max_val=E - 1)
                    slot_tile(j, j % 2, j // 2 if j + 2 < SLOT_TILES else None, e)

        @block.vector
        def _(dve):
            chain = Chain(dve, s_dve)
            GE = NT * E

            def norm_group(g):
                dve.wait_ge(s_x[g], 16)
                for k in range(GROUP):
                    t = g * GROUP + k
                    ins = dve.bn_stats(stats[:, k * 6:k * 6 + 6], xn[:, t * D:(t + 1) * D])
                chain(ins)
                for k in range(GROUP):
                    ins = dve.bn_aggr(moments[:, 2 * k:2 * k + 2], stats[:, k * 6:k * 6 + 6])
                ins.then_inc(s_sqrt_in, 1)

            def scale_and_shift(g):
                of_group = slice(g * GROUP, (g + 1) * GROUP)
                dve.wait_ge(s_sqrt, g + 1)
                chain(dve.reciprocal(rstd[:, of_group], rstd[:, of_group]))
                dve.scalar_tensor_tensor(out=shift[:, of_group], in0=moments[:, 0::2], scalar=-1.0, in1=rstd[:, of_group],
                                         op0=ALU.mult, op1=ALU.mult).then_inc(s_scaling, 1)

            norm_group(0)
            dve.wait_ge(s_dst, 32)
            dve.tensor_copy(dstf, dst_sb).then_inc(s_dstf, 1)
            chain(dve.tensor_tensor(falls, dst_sb, next_dst, ALU.is_gt))
            dve.tensor_reduce(fall_count, falls, AX_X, ALU.add).then_inc(s_falls, 1)
            scale_and_shift(0)
            norm_group(1)
            dve.memset(src_sb[:, STEPS:COLS], 0)
            scale_and_shift(1)
            CH = ET // 4
            for n in range(4):
                dve.wait_ge(s_bcast, n + 1)
                ins = dve.tensor_copy(lo_sb[:, NT - 1 + n * CH:NT - 1 + (n + 1) * CH], bank[n][:, 0:CH])
            chain(ins)
            chain(dve.tensor_scalar(lo_sb[:, NT - 1:STEPS], lo_sb[:, NT - 1:STEPS], 7, None, ALU.arith_shift_right))
            lo_f = gathered[:, 0:7, :].rearrange("p r d -> p (r d)")[:, 0:ET]
            chain(dve.tensor_copy(lo_f, lo_sb[:, NT - 1:STEPS]))
            dve.scalar_tensor_tensor(out=rel_sb[:, NT - 1:STEPS], in0=lo_f, scalar=-128.0, in1=dstf, op0=ALU.mult, op1=ALU.add)
            junk = gathered[:, 7:14, :].rearrange("p r d -> p (r d)")[0:NT - 1, 0:ET]
            cnt, base, dead = (border[0:NT - 1, 3 * P + n:3 * P + n + 1] for n in range(3))
            dve.wait_ge(s_const, 16)
            border_of = const[0:NT - 1, 4 * P:4 * P + 1]
            chain(dve.tensor_scalar(junk, lo_f[0:NT - 1, :], border_of, None, ALU.is_lt))
            chain(dve.tensor_reduce(cnt, junk, AX_X, ALU.add))
            dve.tensor_scalar(dead, cnt, 0.5, 65536.0, ALU.is_lt, ALU.mult)
            dve.tensor_scalar(border_at[0:NT - 1, :], cnt, -1.0, 0.0, ALU.add, ALU.max).then_inc(s_border_at, 1)
            for g in (2, 3):
                norm_group(g)
                scale_and_shift(g)
            dve.wait_ge(s_fall_count, 1)
            dve.tensor_scalar(in_order[:, :], bank[7][:, 0:1], 0.5, None, ALU.is_lt).then_inc(s_order, 1)
            dve.wait_ge(s_border_rows, 48)
            chain(dve.tensor_scalar(base, border_of, -128.0, None, ALU.mult))
            dve.tensor_copy(border[0:NT - 1, 0:P], border_rows[0:NT - 1, 0:P].bitcast(I32))
            dve.tensor_copy(border[0:NT - 1, 2 * P:3 * P], border_rows[0:NT - 1, 2 * P:3 * P])
            chain(dve.tensor_scalar(base, base, dead, None, ALU.add))
            dve.tensor_scalar(border[0:NT - 1, P:2 * P], border_rows[0:NT - 1, P:2 * P].bitcast(I32), base, None, ALU.add).then_inc(s_border_in, 1)
            for g in (4, 5, 6):
                norm_group(g)
                scale_and_shift(g)
            dve.wait_ge(s_scaling, NG)
            for t in range(NT - SHARED, NT):
                rows = xn[:, t * D:(t + 1) * D]
                ins = dve.tensor_scalar(rows, rows, rstd[:, t:t + 1], shift[:, t:t + 1], ALU.mult, ALU.add)
            ins.then_inc(s_xn, 1)
            dve.wait_ge(s_border_t, 3)
            dve.wait_ge(s_edges, 32)
            dve.memset(rel_sb[:, STEPS:COLS], 0.0)
            dve.memset(wgt_sb[:, STEPS:COLS], 0.0)
            dve.tensor_scalar(lo_sb[:, 0:NT - 1], iota[:, 0:NT - 1], 1.0, None, ALU.add)
            dve.tensor_copy(src_sb[:, 0:NT - 1], bank[4][:, 0:NT - 1])
            dve.tensor_copy(rel_sb[:, 0:NT - 1], bank[5][:, 0:NT - 1])
            chain(dve.tensor_copy(wgt_sb[:, 0:NT - 1], bank[6][:, 0:NT - 1]))
            dve.sem_inc(s_added, SUMS)
            dve.sem_inc(s_plan, 1)
            dve.wait_ge(s_agg_clear, 1)

            def build_select(n, k):
                dve.tensor_scalar(select[:, k % SELS, :], iota, rel_sb[:, bass.ds(n, 1)], wgt_sb[:, bass.ds(n, 1)],
                                  ALU.is_equal, ALU.mult).then_inc(s_select, 1)


            def sum_step(i, k, tile):
                dve.wait_ge(s_partial, i * RING + k + RING)
                build_select(i * RING + k + SELS - 1, k + SELS - 1)
                dve.wait_ge(s_added, i * RING + k + SUMS)
                dve.wait_ge(s_partial, i * RING + k + RING + 1)
                rows = agg[:, bass.ds(tile * D, D)]
                dve.tensor_tensor(rows, rows, bank[k % SUMS][:, 0:D], ALU.add).then_inc(s_added, 1)

            def node_tile(t):
                own = Chain(dve, s_node)
                own.enter(t, PER_TILE)

                def moments_of(view):
                    own(dve.bn_stats(n_stats, view))
                    dve.sem_inc(s_spare, 1)
                    dve.bn_aggr(n_moments, n_stats).then_inc(s_var, 1)

                def normalise(dst, src, n):
                    dve.wait_ge(s_dev, t * 4 + n + 1)
                    own(dve.reciprocal(n_rstd, n_rstd))
                    return dve.tensor_scalar(dst, src, n_moments[:, 0:1], n_rstd, ALU.subtract, ALU.mult)

                yield 1
                cols = bass.ds(t * D, D)
                dve.scalar_tensor_tensor(out=h0, in0=xn[:, cols], scalar=eps_col, in1=agg[:, cols], op0=ALU.mult, op1=ALU.add).then_inc(s_h0, 1)
                yield 5
                dve.wait_ge(s_m1, t + 1)
                own(dve.tensor_tensor(hidden, bank[5][:, 0:HID], b1_row, ALU.add))
                yield 1
                moments_of(hidden)
                yield 2
                normalise(hidden, hidden, 0).then_inc(s_z1, 1)
                yield 8
                dve.wait_ge(s_m2, t + 1)
                own(dve.tensor_tensor(second, bank[7][:, 0:D], b2_row, ALU.add))
                moments_of(second)
                yield 2
                own(normalise(second, second, 1))
                own(dve.tensor_tensor(second, second, g2_row, ALU.mult))
                yield 1
                own(dve.tensor_tensor(second, second, beta2_row, ALU.add))
                dve.wait_ge(s_xg, t * 16 + 16)
                dve.scalar_tensor_tensor(out=x_tile, in0=second, scalar=0.0, in1=x_tile, op0=ALU.max, op1=ALU.add).then_inc(s_x1, 1)
                yield 1
                dve.wait_ge(s_x1, t + 1)
                moments_of(x_tile)
                yield 2
                normalise(normed, x_tile, 2).then_inc(s_y, 1)
                yield 1
                dve.wait_ge(s_y, t + 1)
                moments_of(normed)
                yield 2
                normalise(agg[:, cols], normed, 3)
                yield 2
                dve.wait_ge(s_lg, t + 1)
                dve.tensor_tensor(logits[:, bass.ds(t * E, E)], bank[5][:, 0:E], br_row, ALU.add).then_inc(s_lt, 1)
                assert own.n == PER_TILE, own.n

            def tiles_of(i):
                return nc.values_load_multi_w_load_instructions(
                    lo_sb[0:1, bass.ds(i * RING, RING)], engines=[DVE], min_val=0, max_val=NT - 1,
                    skip_runtime_bounds_check_because="node numbers are below the padded count")[1]

            tiles_done = dve.alloc_register("tiles_done_dve")
            dve.reg_mov(tiles_done, 0)
            dve.wait_ge(s_order, 1)
            order = dve.value_load(in_order[0:1, 0:1], min_val=0, max_val=1)
            with dve.If_lt(tiles_done, order):
                for n in range(SELS - 1):
                    build_select(n, n)
                with dve.Fori(0, BORDER_PASSES) as i:
                    tiles = tiles_of(i)
                    for k in range(RING):
                        sum_step(i, k, tiles[k])
                dve.wait_ge(s_param, 16 * PARAMS)
                def spread(passes):
                    steps, tiles = len(passes) * RING, []

                    def step(n):
                        if n % RING == 0 and n > 0:
                            tiles[:] = tiles_of(passes[n // RING])
                        sum_step(passes[n // RING], n % RING, tiles[n % RING])

                    first_tiles = tiles_of(passes[0])
                    with dve.If_lt(tiles_done, first_tiles[0]):
                        tiles[:] = first_tiles
                        interleave(node_tile(dve.snap(tiles_done, min_val=0, max_val=NT - 1)), step, steps, SPAN // steps)
                        dve.reg_add(tiles_done, tiles_done, 1)
                    with dve.Else():
                        tiles[:] = first_tiles
                        for n in range(steps):
                            step(n)

                with dve.Fori(0, SPANS) as i:
                    spread([i * 2 + BORDER_PASSES, i * 2 + (BORDER_PASSES + 1)])
                for i in range(PASSES - REST_PASSES, PASSES):
                    spread([i])
                dve.wait_ge(s_added, SUMS + STEPS)
                dve.wait_ge(s_staged, STEPS // SPAN + 1)
            with dve.Else():
                dve.wait_ge(s_param, 16 * PARAMS)
                dve.sem_inc(s_any_free, 1)
                with dve.Fori(0, ET) as t:
                    own = Chain(dve, s_any_own)
                    own.enter(t, 1 + 2 * NT)
                    own(dve.tensor_copy(rel_now, dstf[:, bass.ds(t, 1)]))
                    dve.sem_inc(s_spare, 1)
                    with dve.Fori(0, NT) as n:
                        dve.tensor_scalar(select[:, 0, :], iota, rel_now, wgt_sb[:, bass.ds(t + (NT - 1), 1)],
                                          ALU.is_equal, ALU.mult).then_inc(s_any_select, 1)
                        dve.wait_ge(s_any_select, t * NT + n + 1)
                        dve.tensor_scalar(rel_now, rel_now, -float(P), None, ALU.add).then_inc(s_any_own, 1)
                        dve.wait_ge(s_any_partial, t * NT + n + 1)
                        rows = agg[:, bass.ds(n * D, D)]
                        dve.tensor_tensor(rows, rows, bank[0][:, 0:D], ALU.add).then_inc(s_any_own, 1)
                        dve.wait_ge(s_any_own, t * (1 + 2 * NT) + n * 2 + 3)
                    dve.sem_inc(s_any_free, 1)

            def rest_of_tiles(first, end):
                with dve.Fori(first, end):
                    with dve.If_lt(tiles_done, NT):
                        for _ in node_tile(dve.snap(tiles_done, min_val=0, max_val=NT - 1)):
                            pass
                        dve.reg_add(tiles_done, tiles_done, 1)

            rest_of_tiles(0, TAIL_TILES)
            with dve.If_lt(tiles_done, NT):
                rest_of_tiles(TAIL_TILES, NT)
            dve.wait_ge(s_lt, NT)

            def te(view):
                return view.rearrange("p (t e) -> p t e", e=E)

            def over_experts(per_tok):
                return per_tok.rearrange("p (t e) -> p t e", e=1).to_broadcast([P, NT, E])

            def over_tokens(per_e):
                return per_e.rearrange("p (t e) -> p t e", t=1).to_broadcast([P, NT, E])

            top, total, key_top, denom = per_token
            chain(dve.tensor_reduce(top, te(logits[:, :]), AX_X, ALU.max))
            dve.tensor_tensor(te(work), te(logits[:, :]), over_experts(top), ALU.subtract).then_inc(s_shift, 1)
            rank = ahead[4]
            chain(dve.tensor_scalar(rank, iota[:, 0:E], -1.0, float(E), ALU.mult, ALU.add))
            dve.wait_ge(s_exp, 1)
            chain(dve.tensor_reduce(total, te(scores), AX_X, ALU.add))
            chain(dve.reciprocal(total, total))
            chain(dve.tensor_tensor(te(scores), te(scores), over_experts(total), ALU.mult))
            for c, onehot in enumerate((onehot0, onehot1)):
                weight = share[:, c * NT:(c + 1) * NT]
                chain(dve.tensor_reduce(weight, te(scores), AX_X, ALU.max))
                chain(dve.tensor_tensor(te(work), te(scores), over_experts(weight), ALU.is_equal))
                chain(dve.tensor_tensor(te(work), te(work), over_tokens(rank), ALU.mult))
                chain(dve.tensor_reduce(key_top, te(work), AX_X, ALU.max))
                chain(dve.tensor_tensor(te(onehot), te(work), over_experts(key_top), ALU.is_equal))
                if c == 0:
                    chain(dve.scalar_tensor_tensor(out=scores, in0=onehot, scalar=-2.0, in1=scores, op0=ALU.mult, op1=ALU.add))
            dve.tensor_tensor(both, onehot0, onehot1, ALU.add).then_inc(s_both, 1)
            chain(dve.tensor_tensor(denom, share[:, 0:NT], share[:, NT:2 * NT], ALU.add))
            chain(dve.reciprocal(denom, denom))
            for c in range(ROUTED):
                dve.tensor_tensor(share[:, c * NT:(c + 1) * NT], share[:, c * NT:(c + 1) * NT], denom, ALU.mult)
            dve.wait_ge(s_count, 2)
            chain(dve.tensor_copy(running, bank[1][:, 0:GE]))
            src_buf, dst_buf = running, other
            step = 1
            while step < NT:
                dve.tensor_copy(dst_buf[:, 0:step * E], src_buf[:, 0:step * E])
                chain(dve.tensor_tensor(dst_buf[:, step * E:GE], src_buf[:, step * E:GE], src_buf[:, 0:GE - step * E], ALU.add))
                src_buf, dst_buf = dst_buf, src_buf
                step *= 2
            tiles_f, tiles_i, end, end2 = ahead[:4]
            chain(dve.tensor_scalar(tiles_i.bitcast(I32), src_buf[:, GE - E:GE], float(P - 1), None, ALU.add))
            chain(dve.tensor_scalar(tiles_i.bitcast(I32), tiles_i.bitcast(I32), 7, None, ALU.arith_shift_right))
            chain(dve.tensor_copy(tiles_f, tiles_i.bitcast(I32)))
            a, b = tiles_f, end
            step = 1
            spare = [end, end2, tiles_i]
            for dst in spare:
                dve.tensor_copy(dst[:, 0:step], a[:, 0:step])
                chain(dve.tensor_tensor(dst[:, step:E], a[:, step:E], a[:, 0:E - step], ALU.add))
                a, step = dst, step * 2
            ends_e = a
            start_e = end
            chain(dve.tensor_tensor(start_e, ends_e, tiles_f, ALU.subtract))
            chain(dve.tensor_scalar(start_e, start_e, float(P), None, ALU.mult))
            dve.wait_ge(s_rows_stored, 16 * NT)
            chain(dve.tensor_tensor(dst_buf, src_buf, bank[1][:, 0:GE], ALU.subtract))
            chain(dve.tensor_tensor(dst_buf, dst_buf, bank[0][:, 0:GE], ALU.add))
            chain(dve.tensor_tensor(te(dst_buf), te(dst_buf), over_tokens(start_e), ALU.add))
            for c, onehot in enumerate((onehot0, onehot1)):
                chain(dve.tensor_tensor(work, onehot, dst_buf, ALU.mult))
                chain(dve.tensor_reduce(slot[:, c * NT:(c + 1) * NT], te(work), AX_X, ALU.add))
            j_of = iota.rearrange("p (j e) -> p j e", e=1).to_broadcast([P, P, E])
            chain(dve.tensor_tensor(ends.rearrange("p (j e) -> p j e", e=E), j_of,
                                    ends_e.rearrange("p (j e) -> p j e", j=1).to_broadcast([P, P, E]), ALU.is_ge))
            chain(dve.tensor_reduce(expert_f, ends.rearrange("p (j e) -> p j e", e=E), AX_X, ALU.add))
            dve.tensor_copy(tiles_used[:, :], ends_e[:, E - 1:E])
            dve.tensor_scalar(tile_expert[:, :], expert_f, float(E - 1), None, ALU.min).then_inc(s_routed, 1)
            dve.wait_ge(s_routed, 1)

            row, col = (row_and_col.rearrange("p (t c k) -> p c t k", c=ROUTED, k=2)[:, :, :, k] for k in range(2))
            dve.tensor_scalar(token_next, iota[:, 0:NT], float(P), const[:, 4 * P:4 * P + 1], ALU.mult, ALU.add)
            chain(dve.tensor_copy(slot_int, slot))
            chain(dve.tensor_scalar(slot_int, slot_int, 7, None, ALU.arith_shift_right))
            chain(dve.tensor_copy(col, slot_int.rearrange("p (c t) -> p c t", c=ROUTED)))
            chain(dve.scalar_tensor_tensor(out=row, in0=col, scalar=-float(P), in1=slot.rearrange("p (c t) -> p c t", c=ROUTED),
                                           op0=ALU.mult, op1=ALU.add))

            def onehots(t, b):
                if not isinstance(t, int) or t >= HOTS:
                    dve.wait_ge(s_used, t - (HOTS - 1))
                dve.tensor_tensor(hot[:, b, :, :, :].rearrange("p c k n -> p (c k) n"),
                                  iota.rearrange("p (m n) -> p m n", m=1).to_broadcast([P, ROUTED * 2, P]),
                                  row_and_col[:, bass.ds(t * (ROUTED * 2), ROUTED * 2)].rearrange("p (m n) -> p m n", n=1).to_broadcast([P, ROUTED * 2, P]),
                                  ALU.is_equal).then_inc(s_hot, 1)

            over_tiles(dve, onehots)
            dve.wait_ge(s_used, NT)
            token_of = bank[6][:, 0:SLOT_TILES]
            dve.tensor_copy(slot_share[:, :], bank[6][:, SLOT_TILES:2 * SLOT_TILES])
            dve.tensor_scalar(slot_from[:, :], token_of, -1.0, 0.0, ALU.add, ALU.max)
            chain(dve.tensor_scalar(empty, token_of, 0.5, const[:, 4 * P:4 * P + 1], ALU.is_lt, ALU.mult))
            chain(dve.scalar_tensor_tensor(out=empty, in0=token_of, scalar=-1.0, in1=empty, op0=ALU.add, op1=ALU.add))
            dve.tensor_scalar(past_nodes, token_of, 0.5, float(NODES), ALU.is_lt, ALU.mult).then_inc(s_slots, 1)
            dve.wait_ge(s_slots, 1)
            dve.tensor_tensor(slot_to[:, :], past_nodes, empty, ALU.add).then_inc(s_slots, 1)


            def scale_rows(j, r, e):
                dve.wait_ge(s_xt, j + 1)
                for c in range(DC):
                    at = bass.ds(e * DC + c, 1)
                    ins = dve.tensor_scalar(xt[:, r, c * P:(c + 1) * P], bank[4][:, c * P:(c + 1) * P], ln_g_col[:, at], ln_b_col[:, at], ALU.mult, ALU.add)
                ins.then_inc(s_xs, 1)

            def place_w1(r, e):
                dve.tensor_copy(w1_now[:, r, :], w1_all[:, bass.ds(e * (DC * FF), DC * FF)]).then_inc(s_w1_now, 1)

            def take_output(j, r, m):
                dve.wait_ge(s_y_free, j + 1)
                dve.wait_ge(s_bias[r], m * 16 + 16)
                dve.wait_ge(s_f2, j + 1)
                dve.tensor_tensor(y_sb[:, r, :], bank[5][:, 0:D], bias[:, r, :], ALU.add).then_inc(s_ys, 1)
                dve.wait_ge(s_ys, j + 2)
                dve.tensor_scalar(y_sb[:, r, :], y_sb[:, r, :], slot_share[:, bass.ds(j, 1)], None, ALU.mult).then_inc(s_yw, 1)

            dve.sem_inc(s_y_free, 2)
            dve.sem_inc(s_ys, 1)
            dve.wait_ge(s_weights, 16 * 2 * E)
            for j in range(LOOKED):
                e = dve.value_load(tile_expert[0:1, j:j + 1], min_val=0, max_val=E - 1)
                place_w1(j, e)
                scale_rows(j, j, e)

            def slot_tile(j, r, m, e_after):
                if e_after is not None:
                    dve.wait_ge(s_f1, j * 2 + 2)
                    dve.sem_inc(s_spare, 1)
                    place_w1(r, e_after)
                    scale_rows(j + 2, r, e_after)
                take_output(j, r, m)

            with dve.Fori(0, PAIRS) as i:
                for r in range(2):
                    e_after = dve.value_load(tile_expert[0:1, bass.ds(i * 2 + (r + LOOKED), 1)], min_val=0, max_val=E - 1)
                    slot_tile(i * 2 + r, r, i, e_after)
            with last_tiles(dve, "dve"):
                for j in range(2 * PAIRS, SLOT_TILES):
                    e_after = dve.value_load(tile_expert[0:1, j + 2:j + 3], min_val=0, max_val=E - 1) if j + 2 < SLOT_TILES else None
                    slot_tile(j, j % 2, j // 2, e_after)


def kernel(**inputs):
    import numpy as np
    import concourse.bacc as bacc
    from concourse.bass_utils import run_bass_kernel_spmd as run

    inp = {k: np.asarray(v) for k, v in inputs.items()}
    N, D = inp["x"].shape
    nodes = -(-N // P) * P
    x = np.zeros((nodes, D), np.float32)
    x[:N] = inp["x"]
    edges = inp["src"].shape[0]
    tiles = -(-edges // (P * RING)) * RING

    def rows(a, fill):
        b = np.full((tiles * P,), fill, a.dtype)
        b[:edges] = a
        return b.reshape(tiles, P)

    src, dst, wgt = rows(inp["src"], 0), rows(inp["dst"], nodes - 1), rows(inp["edge_weight"], 0)
    k = np.arange(P, dtype=np.float32)
    consts = np.concatenate([np.eye(P), k[:, None] < k[None, :], np.tile(k, (P, 1)), np.ones((P, P)), k[:, None] + 1, k[:, None]], axis=1).astype(np.float32)

    def tcol(a, w):
        return np.ascontiguousarray(a.reshape(-1, P).T)

    arrays = {
        "x": x, "src_rows": src, "dst_rows": dst, "weight_rows": wgt,
        "src_cols": np.ascontiguousarray(src.T), "dst_cols": np.ascontiguousarray(dst.T),
        "next_dst_cols": np.append(dst.reshape(-1)[1:], dst[-1, -1:]).reshape(dst.shape).T,
        "weight_cols": np.ascontiguousarray(wgt.T),
        "epsilon": inp["L0_gnn_epsilon"],
        "w1t": np.ascontiguousarray(inp["L0_gnn_w1"].T), "w2t": np.ascontiguousarray(inp["L0_gnn_w2"].T),
        "gnn_rows": np.concatenate([inp["L0_gnn_b1"], inp["L0_gnn_b2"], inp["L0_gnn_g2"], inp["L0_gnn_beta2"]])[None],
        "g1t": tcol(inp["L0_gnn_g1"], 4), "beta1t": tcol(inp["L0_gnn_beta1"], 4),
        "wr": inp["L0_ffn_Wr"], "br": inp["L0_ffn_br"][None],
        "ln_gt": tcol(inp["L0_ffn_ln_g"], 16), "ln_bt": tcol(inp["L0_ffn_ln_b"], 16),
        "expert_w1": inp["L0_ffn_W1"], "expert_w2": inp["L0_ffn_W2"],
        "expert_b1t": tcol(inp["L0_ffn_b1"], 8), "expert_b2": inp["L0_ffn_b2"],
        "consts": consts,
    }
    arrays = {n: np.ascontiguousarray(a) for n, a in arrays.items()}
    nc = bacc.Bacc("TRN2", target_bir_lowering=False, num_devices=1)
    args = [nc.dram_tensor(n, a.shape, mybir.dt.from_np(a.dtype), kind="ExternalInput").ap() for n, a in arrays.items()]
    out = nc.dram_tensor("out", (nodes + P, D), F32, kind="ExternalOutput").ap()
    gnn_moe(nc, *args, out)
    r = run(nc, [arrays], core_ids=[0])
    return r.results[0]["out"][:N]
```
